# Optimizing a Trainium2 kernel written in Bass

```python
import numpy as np
import jax
import jax.numpy as jnp

def _softmax(x, axis=-1):
    return jax.nn.softmax(x, axis=axis)

def _gelu(x):
    return jax.nn.gelu(x, approximate=True)

def _silu(x):
    return jax.nn.silu(x)

def _sigmoid(x):
    return jax.nn.sigmoid(x)

def _layernorm(x, axis=-1, eps=1e-05):
    m = jnp.mean(x, axis=axis, keepdims=True)
    v = jnp.var(x, axis=axis, keepdims=True)
    return (x - m) / jnp.sqrt(v + eps)

def _scatter_add(tgt, idx, src, axis=0):
    return tgt.at[idx].add(src)

def _segment_sum(src, seg, n):
    return jax.ops.segment_sum(src, seg, n)
kernel_name = 'mk_early_fusion_d1_tok_img512_r4_613f12'

def setup_inputs(seed: int=0):
    np.random.seed(seed)
    _w = jnp.asarray

    def _rec_inputs():
        import jax
        import jax.numpy as jnp
        _rk = jax.random.key(seed)
        x = -0.000392918 + 0.999932 * jax.random.normal(jax.random.fold_in(_rk, 1), (16, 1, 128, 128), jnp.float32)
        txt = 0.229487 + 0.681011 * jax.random.normal(jax.random.fold_in(_rk, 2), (16, 512, 128), jnp.float32)
        return (x, txt)
    x, txt = _rec_inputs()

    def _L0_tok_setup():
        import math
        import jax, jax.numpy as jnp
        import numpy as np
        PW = PH = 16
        EMB = 128
        HID = 128
        B, H, W = (64, 128, 128)
        L = H // PW * (W // PH)
        SIGMA_ZERO = 0.1

        def _f_noise(x):
            return jnp.sign(x) * jnp.sqrt(jnp.abs(x))

        def _noisy_linear(x, w, b, sw, sb, eps_in, eps_out):
            ei = _f_noise(eps_in)
            eo = _f_noise(eps_out)
            w_n = w + sw * (eo[:, None] * ei[None, :])
            b_n = b + sb * eo
            return x @ w_n.T + b_n

        def _unfold_patches(x):
            b = x.shape[0]
            p = x.reshape(b, H // PW, PW, W // PH, PH)
            p = p.transpose(0, 1, 3, 2, 4)
            return p.reshape(b, L, PW * PH)

        def _pos_encoding(x):
            pos = jnp.arange(L, dtype=jnp.float32)[:, None]
            div = jnp.exp(jnp.arange(0, EMB, 2, dtype=jnp.float32) * (-math.log(10000.0) / EMB))
            ang = pos * div
            pe = jnp.stack([jnp.sin(ang), jnp.cos(ang)], axis=-1).reshape(L, EMB)
            return x + pe[None, :, :]
        key = jax.random.key(seed)
        ks = jax.random.split(key, 12)
        in_f = PW * PH
        sig = SIGMA_ZERO / math.sqrt(in_f)
        bnd1 = 1.0 / math.sqrt(in_f)
        bnd3 = 1.0 / math.sqrt(HID)
        u = lambda k, shape, bnd: jax.random.uniform(k, shape, jnp.float32, -bnd, bnd)
        return {'inputs': jax.random.normal(ks[0], (B, 1, H, W), jnp.float32), 'W1_w': u(ks[1], (HID, in_f), bnd1), 'W1_b': u(ks[2], (HID,), bnd1), 'W1_sw': jnp.full((HID, in_f), sig, jnp.float32), 'W1_sb': jnp.full((HID,), sig, jnp.float32), 'W2_w': u(ks[3], (HID, in_f), bnd1), 'W2_b': u(ks[4], (HID,), bnd1), 'W2_sw': jnp.full((HID, in_f), sig, jnp.float32), 'W2_sb': jnp.full((HID,), sig, jnp.float32), 'W3_w': u(ks[5], (EMB, HID), bnd3), 'W3_b': u(ks[6], (EMB,), bnd3), 'eps_in1': jax.random.normal(ks[7], (in_f,), jnp.float32), 'eps_out1': jax.random.normal(ks[8], (HID,), jnp.float32), 'eps_in2': jax.random.normal(ks[9], (in_f,), jnp.float32), 'eps_out2': jax.random.normal(ks[10], (HID,), jnp.float32)}
    _L0_tok_all = _L0_tok_setup()
    _L0_tok_in = {k: v for k, v in _L0_tok_all.items() if k in ('W1_w', 'W1_b', 'W1_sw', 'W1_sb', 'W2_w', 'W2_b', 'W2_sw', 'W2_sb', 'W3_w', 'W3_b', 'eps_in1', 'eps_out1', 'eps_in2', 'eps_out2')}
    del _L0_tok_all

    def _L0_attn_setup():
        import jax, jax.numpy as jnp
        import numpy as np
        import math
        D_MODEL = 128
        NUM_HEADS = 8
        B, L = (2, 1024)
        EPS_NORM = 1e-08
        PLASTICITY = 1.0

        def _hebbian_forward(x, qkv_w, qkv_b, out_w, out_b, decay_w, decay_b, norm_scale):
            Bsz, Lsz, D = x.shape
            H = NUM_HEADS
            E = D // H
            qkv = x @ qkv_w.T + qkv_b
            q, k, v = jnp.split(qkv, 3, axis=-1)
            q = q.reshape(Bsz, Lsz, H, E)
            k = k.reshape(Bsz, Lsz, H, E)
            v = v.reshape(Bsz, Lsz, H, E)
            q = (jax.nn.elu(q) + 1.0) / math.sqrt(E)
            k = jax.nn.elu(k) + 1.0
            decay_logits = x @ decay_w.T + decay_b
            lambdas = (0.9 + 0.1 * jax.nn.sigmoid(decay_logits)) * PLASTICITY
            log_lambdas = jnp.log(jnp.clip(lambdas, 1e-06))[..., None]
            log_lambda_cum = jnp.clip(jnp.cumsum(log_lambdas, axis=1), -50.0, 50.0)
            decay_k = jnp.exp(-log_lambda_cum)
            decay_q = jnp.exp(log_lambda_cum)
            k_decayed = k * decay_k
            q_decayed = q * decay_q
            kv = jnp.einsum('blhe,blhf->blhef', k_decayed, v)
            memory_state = jnp.cumsum(kv, axis=1)
            k_sum_decayed = jnp.cumsum(k_decayed, axis=1)
            num = jnp.einsum('blhe,blhef->blhf', q_decayed, memory_state)
            den = jnp.einsum('blhe,blhe->blh', q_decayed, k_sum_decayed)[..., None] + 1e-06
            out = (num / den).reshape(Bsz, Lsz, D)
            out = out @ out_w.T + out_b
            rnorm = jax.lax.rsqrt(jnp.mean(out * out, axis=-1, keepdims=True) + EPS_NORM)
            return out * rnorm * norm_scale
        key = jax.random.key(seed)
        ks = jax.random.split(key, 6)
        D, H = (D_MODEL, NUM_HEADS)
        std = 1.0 / math.sqrt(D)
        x = jax.random.normal(ks[0], (B, L, D), dtype=jnp.float32)
        qkv_w = jax.random.normal(ks[1], (3 * D, D), dtype=jnp.float32) * std
        qkv_b = jnp.zeros((3 * D,), dtype=jnp.float32)
        out_w = jax.random.normal(ks[2], (D, D), dtype=jnp.float32) * std
        out_b = jnp.zeros((D,), dtype=jnp.float32)
        decay_w = jax.random.normal(ks[3], (H, D), dtype=jnp.float32) * 0.02
        decay_b = jnp.full((H,), 4.0, dtype=jnp.float32)
        norm_scale = jnp.ones((D,), dtype=jnp.float32)
        return {'x': x, 'qkv_w': qkv_w, 'qkv_b': qkv_b, 'out_w': out_w, 'out_b': out_b, 'decay_w': decay_w, 'decay_b': decay_b, 'norm_scale': norm_scale}
    _L0_attn_all = _L0_attn_setup()
    _L0_attn_in = {k: v for k, v in _L0_attn_all.items() if k in ('qkv_w', 'qkv_b', 'out_w', 'out_b', 'decay_w', 'decay_b', 'norm_scale')}
    del _L0_attn_all

    def _L0_ffn_setup():
        import jax, jax.numpy as jnp
        import numpy as np
        MARK_AX, OP_ADD, OP_SUB = (0, 1, 2)
        ALU_LO, ALU_HI = (16, 32)
        AX_CARRY_LO, AX_CARRY_HI = (48, 64)
        OPCODE_BASE = 80
        OUTPUT_LO, OUTPUT_HI, CARRY = (128, 144, 160)
        NIB_A, NIB_B, OP_START = (0, 1, 10)
        RESULT, CARRY_OUT = (100, 101)
        GE_POS, GE_DIM = (8, 160)
        OPC_ADD, OPC_SUB = (25, 26)
        B, S, D = (8, 1024, 128)

        def _decode_nibble(x, base):
            return jnp.argmax(x[..., base:base + 16] > 0.5, axis=-1).astype(x.dtype)

        def _pipeline(h, W, b):
            for i in range(3):
                h = jnp.einsum('bspd,od->bspo', h, W[i]) + b[i]
                if i < 2:
                    h = jax.nn.relu(h)
            return h
        key = jax.random.key(seed)
        kx, k1, k2, k3, k4 = jax.random.split(key, 5)
        x_bd = jax.random.uniform(kx, (B, S, D), dtype=jnp.float32)
        Wa = jax.random.normal(k1, (3, GE_DIM, GE_DIM), dtype=jnp.float32) * 0.05
        ba = jax.random.normal(k2, (3, GE_DIM), dtype=jnp.float32) * 0.05
        Ws = jax.random.normal(k3, (3, GE_DIM, GE_DIM), dtype=jnp.float32) * 0.05
        bs = jax.random.normal(k4, (3, GE_DIM), dtype=jnp.float32) * 0.05
        return {'x_bd': x_bd, 'Wa': Wa, 'ba': ba, 'Ws': Ws, 'bs': bs}
    _L0_ffn_all = _L0_ffn_setup()
    _L0_ffn_in = {k: v for k, v in _L0_ffn_all.items() if k in ('Wa', 'ba', 'Ws', 'bs')}
    del _L0_ffn_all
    return {'x': x, 'txt': txt, 'L0_tok_W1_w': _L0_tok_in['W1_w'], 'L0_tok_W1_b': _L0_tok_in['W1_b'], 'L0_tok_W1_sw': _L0_tok_in['W1_sw'], 'L0_tok_W1_sb': _L0_tok_in['W1_sb'], 'L0_tok_W2_w': _L0_tok_in['W2_w'], 'L0_tok_W2_b': _L0_tok_in['W2_b'], 'L0_tok_W2_sw': _L0_tok_in['W2_sw'], 'L0_tok_W2_sb': _L0_tok_in['W2_sb'], 'L0_tok_W3_w': _L0_tok_in['W3_w'], 'L0_tok_W3_b': _L0_tok_in['W3_b'], 'L0_tok_eps_in1': _L0_tok_in['eps_in1'], 'L0_tok_eps_out1': _L0_tok_in['eps_out1'], 'L0_tok_eps_in2': _L0_tok_in['eps_in2'], 'L0_tok_eps_out2': _L0_tok_in['eps_out2'], 'L0_attn_qkv_w': _L0_attn_in['qkv_w'], 'L0_attn_qkv_b': _L0_attn_in['qkv_b'], 'L0_attn_out_w': _L0_attn_in['out_w'], 'L0_attn_out_b': _L0_attn_in['out_b'], 'L0_attn_decay_w': _L0_attn_in['decay_w'], 'L0_attn_decay_b': _L0_attn_in['decay_b'], 'L0_attn_norm_scale': _L0_attn_in['norm_scale'], 'L0_ffn_Wa': _L0_ffn_in['Wa'], 'L0_ffn_ba': _L0_ffn_in['ba'], 'L0_ffn_Ws': _L0_ffn_in['Ws'], 'L0_ffn_bs': _L0_ffn_in['bs']}

def reference(x, txt, L0_tok_W1_w, L0_tok_W1_b, L0_tok_W1_sw, L0_tok_W1_sb, L0_tok_W2_w, L0_tok_W2_b, L0_tok_W2_sw, L0_tok_W2_sb, L0_tok_W3_w, L0_tok_W3_b, L0_tok_eps_in1, L0_tok_eps_out1, L0_tok_eps_in2, L0_tok_eps_out2, L0_attn_qkv_w, L0_attn_qkv_b, L0_attn_out_w, L0_attn_out_b, L0_attn_decay_w, L0_attn_decay_b, L0_attn_norm_scale, L0_ffn_Wa, L0_ffn_ba, L0_ffn_Ws, L0_ffn_bs):
    import jax
    import jax.numpy as jnp

    def _L0_tok_ref(inputs, W1_w, W1_b, W1_sw, W1_sb, W2_w, W2_b, W2_sw, W2_sb, W3_w, W3_b, eps_in1, eps_out1, eps_in2, eps_out2):
        import math
        import jax, jax.numpy as jnp
        import numpy as np
        PW = PH = 16
        EMB = 128
        HID = 128
        B, H, W = (64, 128, 128)
        L = H // PW * (W // PH)
        SIGMA_ZERO = 0.1

        def _f_noise(x):
            return jnp.sign(x) * jnp.sqrt(jnp.abs(x))

        def _noisy_linear(x, w, b, sw, sb, eps_in, eps_out):
            ei = _f_noise(eps_in)
            eo = _f_noise(eps_out)
            w_n = w + sw * (eo[:, None] * ei[None, :])
            b_n = b + sb * eo
            return x @ w_n.T + b_n

        def _unfold_patches(x):
            b = x.shape[0]
            p = x.reshape(b, H // PW, PW, W // PH, PH)
            p = p.transpose(0, 1, 3, 2, 4)
            return p.reshape(b, L, PW * PH)

        def _pos_encoding(x):
            pos = jnp.arange(L, dtype=jnp.float32)[:, None]
            div = jnp.exp(jnp.arange(0, EMB, 2, dtype=jnp.float32) * (-math.log(10000.0) / EMB))
            ang = pos * div
            pe = jnp.stack([jnp.sin(ang), jnp.cos(ang)], axis=-1).reshape(L, EMB)
            return x + pe[None, :, :]
        x = _unfold_patches(inputs)
        g = _noisy_linear(x, W1_w, W1_b, W1_sw, W1_sb, eps_in1, eps_out1)
        x_gate = g * jnp.tanh(jax.nn.softplus(g))
        x_inner = _noisy_linear(x, W2_w, W2_b, W2_sw, W2_sb, eps_in2, eps_out2)
        x = x_gate * x_inner
        x = x @ W3_w.T + W3_b
        return _pos_encoding(x)

    def _L0_attn_ref(x, qkv_w, qkv_b, out_w, out_b, decay_w, decay_b, norm_scale):
        import jax, jax.numpy as jnp
        import numpy as np
        import math
        D_MODEL = 128
        NUM_HEADS = 8
        B, L = (2, 1024)
        EPS_NORM = 1e-08
        PLASTICITY = 1.0

        def _hebbian_forward(x, qkv_w, qkv_b, out_w, out_b, decay_w, decay_b, norm_scale):
            Bsz, Lsz, D = x.shape
            H = NUM_HEADS
            E = D // H
            qkv = x @ qkv_w.T + qkv_b
            q, k, v = jnp.split(qkv, 3, axis=-1)
            q = q.reshape(Bsz, Lsz, H, E)
            k = k.reshape(Bsz, Lsz, H, E)
            v = v.reshape(Bsz, Lsz, H, E)
            q = (jax.nn.elu(q) + 1.0) / math.sqrt(E)
            k = jax.nn.elu(k) + 1.0
            decay_logits = x @ decay_w.T + decay_b
            lambdas = (0.9 + 0.1 * jax.nn.sigmoid(decay_logits)) * PLASTICITY
            log_lambdas = jnp.log(jnp.clip(lambdas, 1e-06))[..., None]
            log_lambda_cum = jnp.clip(jnp.cumsum(log_lambdas, axis=1), -50.0, 50.0)
            decay_k = jnp.exp(-log_lambda_cum)
            decay_q = jnp.exp(log_lambda_cum)
            k_decayed = k * decay_k
            q_decayed = q * decay_q
            kv = jnp.einsum('blhe,blhf->blhef', k_decayed, v)
            memory_state = jnp.cumsum(kv, axis=1)
            k_sum_decayed = jnp.cumsum(k_decayed, axis=1)
            num = jnp.einsum('blhe,blhef->blhf', q_decayed, memory_state)
            den = jnp.einsum('blhe,blhe->blh', q_decayed, k_sum_decayed)[..., None] + 1e-06
            out = (num / den).reshape(Bsz, Lsz, D)
            out = out @ out_w.T + out_b
            rnorm = jax.lax.rsqrt(jnp.mean(out * out, axis=-1, keepdims=True) + EPS_NORM)
            return out * rnorm * norm_scale
        return _hebbian_forward(x, qkv_w, qkv_b, out_w, out_b, decay_w, decay_b, norm_scale)

    def _L0_ffn_ref(x_bd, Wa, ba, Ws, bs):
        import jax, jax.numpy as jnp
        import numpy as np
        MARK_AX, OP_ADD, OP_SUB = (0, 1, 2)
        ALU_LO, ALU_HI = (16, 32)
        AX_CARRY_LO, AX_CARRY_HI = (48, 64)
        OPCODE_BASE = 80
        OUTPUT_LO, OUTPUT_HI, CARRY = (128, 144, 160)
        NIB_A, NIB_B, OP_START = (0, 1, 10)
        RESULT, CARRY_OUT = (100, 101)
        GE_POS, GE_DIM = (8, 160)
        OPC_ADD, OPC_SUB = (25, 26)
        B, S, D = (8, 1024, 128)

        def _decode_nibble(x, base):
            return jnp.argmax(x[..., base:base + 16] > 0.5, axis=-1).astype(x.dtype)

        def _pipeline(h, W, b):
            for i in range(3):
                h = jnp.einsum('bspd,od->bspo', h, W[i]) + b[i]
                if i < 2:
                    h = jax.nn.relu(h)
            return h
        x = x_bd
        Bsz, seq, _ = x.shape
        x_ge = jnp.zeros((Bsz, seq, GE_POS, GE_DIM), dtype=x.dtype)
        x_ge = x_ge.at[..., 0, NIB_A].set(_decode_nibble(x, ALU_LO))
        x_ge = x_ge.at[..., 1, NIB_A].set(_decode_nibble(x, ALU_HI))
        x_ge = x_ge.at[..., 0, NIB_B].set(_decode_nibble(x, AX_CARRY_LO))
        x_ge = x_ge.at[..., 1, NIB_B].set(_decode_nibble(x, AX_CARRY_HI))
        x_ge = x_ge.at[..., :, OP_START + OPC_ADD].set(x[..., OPCODE_BASE + OPC_ADD][..., None])
        x_ge = x_ge.at[..., :, OP_START + OPC_SUB].set(x[..., OPCODE_BASE + OPC_SUB][..., None])
        mark = x[..., MARK_AX] > 0.5
        m_add = mark & (x[..., OP_ADD] > 0.5)
        m_sub = mark & ~(x[..., OP_ADD] > 0.5) & (x[..., OP_SUB] > 0.5)
        active = (m_add | m_sub).astype(x.dtype)
        y_add = _pipeline(x_ge, Wa, ba)
        y_sub = _pipeline(x_ge, Ws, bs)
        y = jnp.where(m_add[..., None, None], y_add, jnp.where(m_sub[..., None, None], y_sub, x_ge))
        res_lo = jnp.clip(jnp.round(y[..., 0, RESULT]), 0, 15).astype(jnp.int32)
        res_hi = jnp.clip(jnp.round(y[..., 1, RESULT]), 0, 15).astype(jnp.int32)
        oh_lo = jax.nn.one_hot(res_lo, 16, dtype=x.dtype) * active[..., None]
        oh_hi = jax.nn.one_hot(res_hi, 16, dtype=x.dtype) * active[..., None]
        carry = (jnp.round(y[..., 1, CARRY_OUT]) > 0.5).astype(x.dtype) * active
        out = x
        out = out.at[..., OUTPUT_LO:OUTPUT_LO + 16].add(2.0 * oh_lo)
        out = out.at[..., OUTPUT_HI:OUTPUT_HI + 16].add(2.0 * oh_hi)
        out = out.at[..., CARRY].add(carry)
        return out
    h = _L0_tok_ref(x, L0_tok_W1_w, L0_tok_W1_b, L0_tok_W1_sw, L0_tok_W1_sb, L0_tok_W2_w, L0_tok_W2_b, L0_tok_W2_sw, L0_tok_W2_sb, L0_tok_W3_w, L0_tok_W3_b, L0_tok_eps_in1, L0_tok_eps_out1, L0_tok_eps_in2, L0_tok_eps_out2)
    h = jnp.concatenate([h, txt], axis=1)
    h = h + _L0_attn_ref(_layernorm(h, axis=-1), L0_attn_qkv_w, L0_attn_qkv_b, L0_attn_out_w, L0_attn_out_b, L0_attn_decay_w, L0_attn_decay_b, L0_attn_norm_scale)
    h = h + _L0_ffn_ref(_layernorm(h, axis=-1), L0_ffn_Wa, L0_ffn_ba, L0_ffn_Ws, L0_ffn_bs)
    return h

_drawn_inputs = setup_inputs


def setup_inputs(seed=0):
    import zlib

    import numpy as np

    out = dict(_drawn_inputs(seed))
    spreads = {'L0_tok_W1_sw': (0.0062500000931322575, 0.6),
     'L0_tok_W1_sb': (0.0062500000931322575, 0.6),
     'L0_tok_W2_sw': (0.0062500000931322575, 0.6),
     'L0_tok_W2_sb': (0.0062500000931322575, 0.6),
     'L0_attn_qkv_b': (0.0, 0.1),
     'L0_attn_out_b': (0.0, 0.1),
     'L0_attn_decay_b': (4.0, 0.2),
     'L0_attn_norm_scale': (1.0, 0.2)}
    factors = {'L0_tok_W1_b': 8.0,
     'L0_tok_W2_b': 8.0,
     'L0_tok_eps_in1': 8.0,
     'L0_tok_eps_out1': 8.0,
     'L0_tok_eps_in2': 7.897,
     'L0_tok_eps_out2': 7.86,
     'L0_attn_decay_w': 8.0}
    for name, (base, spread) in spreads.items():
        noise = np.random.default_rng([zlib.crc32(name.encode()), seed]).standard_normal(out[name].shape)
        drawn = base * np.exp(spread * noise) if base else spread * noise
        out[name] = jnp.asarray(drawn.astype(out[name].dtype))
    for name, factor in factors.items():
        out[name] = (out[name] * factor).astype(out[name].dtype)
    return out
```

```python
from contextlib import ExitStack

import numpy as np

import concourse.bass as bass
from concourse import mybir

F32 = mybir.dt.float32
BF16 = mybir.dt.bfloat16
ALU = mybir.AluOpType
ACT = mybir.ActivationFunctionType

P = 128
BATCHES = 16
PAIRS = BATCHES // 2
D = 128
H = 8
E = D // H
C = 64
TEXT = 512
CHUNKS = (C + TEXT) // C
TILES = 3
GROUPS = CHUNKS // TILES
GT = TILES * P
VD = D + H
W1E = E + 1
SV = H * W1E
H_RING = 2 * GROUPS
PIX = 256
LN_EPS = 1e-5
RMS_EPS = 1e-8
DEN_EPS = 1e-6 * E ** 0.5

CST = {"U": (0, P), "ones": (P, P), "ident": (2 * P, P), "mask": (3 * P, C), "blocks": (3 * P + C, SV),
       "pos": (3 * P + C + SV, P)}
CST_N = 3 * P + C + SV + P
WTS = {"wq": (0, D), "wk": (D, D), "wvd": (2 * D, VD), "wo": (2 * D + VD, D), "w3": (3 * D + VD, D)}
WTS_N = 4 * D + VD
COL = {n: i for i, n in enumerate(["bq", "bk", "b1", "sb1", "eo1", "b2", "sb2", "eo2",
                                   "ei1a", "ei1b", "ei2a", "ei2b"])}
ROW = {"vd": (0, VD), "o": (VD, D), "w3": (VD + D, D), "ns": (VD + 2 * D, D), "eo1": (VD + 3 * D, D),
       "eo2": (VD + 4 * D, D)}
ROW_N = VD + 5 * D


def build(nc, txt, patches, cst_in, wts_in, noisy_w, noisy_sw, cols_in, rows_in, out):
    with ExitStack() as ctx:
        def sb(name, shape, dt=F32):
            return ctx.enter_context(nc.sbuf_tensor(name, shape, dt))

        def ps(name, shape):
            return ctx.enter_context(nc.psum_tensor(name, shape, F32))

        def sem(name):
            return ctx.enter_context(nc.semaphore(name))

        cst = sb("cst", [P, CST_N])
        wts = sb("wts", [P, WTS_N])
        w12 = sb("w12", [P, 4, D])
        sw12 = sb("sw12", [P, 4, D])
        nz12 = sb("nz12", [P, 4, D])
        cols = sb("cols", [P, len(COL)])
        rows = sb("rows", [P, ROW_N])
        pix = sb("pix", [P, 2, BATCHES * C])
        cst_of = {n: cst[:, a:a + w] for n, (a, w) in CST.items()}
        w_of = {n: wts[:, a:a + w] for n, (a, w) in WTS.items()}
        row_of = {n: rows[:, a:a + w] for n, (a, w) in ROW.items()}
        col = {n: cols[:, i:i + 1] for n, i in COL.items()}
        roots = sb("roots", [P, 6 + 2 * D])
        rootn = sb("rootn", [P, 6 + 2 * D])
        noise = sb("noise", [P, 6 + 2 * D])
        epsv = sb("epsv", [P, 6 + 2 * D])
        bias12 = sb("bias12", [P, 2])
        minus_half = sb("minus_half", [P, TILES])
        ones_b = sb("ones_b", [P, P], BF16)
        BR = VD + 2 * D
        part = [sb(f"part{i}", [P, BR], BF16) for i in range(3)]
        rest = [sb(f"rest{i}", [P, BR]) for i in range(2)]
        bias_vd = sb("bias_vd", [P, TILES, VD], BF16)
        bias_o = sb("bias_o", [P, 2, D], BF16)
        ge = sb("ge", [P, 512])
        gl = sb("gl", [P, 512])
        gn = sb("gn", [P, 512])
        gr = sb("gr", [P, 512])
        gm = sb("gm", [P, 512])
        u = sb("u", [P, 2, 512])
        himg = sb("himg", [P, PAIRS, D])

        def ring(name, shape, dt=F32):
            return [sb(f"{name}{g}", shape, dt) for g in range(GROUPS)]

        h = [sb(f"h{i}", [P, TILES, D]) for i in range(H_RING)]
        stat = ring("stat", [P, TILES, 6])
        mv = ring("mv", [P, TILES, 2])
        ve = ring("ve", [P, 2, TILES])
        rn = ring("rn", [P, 2, TILES])
        xn = ring("xn", [P, TILES, D])
        xT = ring("xT", [P, GT])
        eq = ring("eq", [P, GT])
        rq = ring("rq", [P, GT])
        ek = ring("ek", [P, GT])
        rk = ring("rk", [P, GT])
        q = ring("q", [P, GT])
        k = ring("k", [P, GT])
        qbd = ring("qbd", [P, H, GT])
        ez = ring("ez", [P, TILES, H])
        eu = ring("eu", [P, TILES, H])
        er = ring("er", [P, TILES, H])
        lam = ring("lam", [P, TILES, H])
        L = ring("L", [P, TILES, H])
        before = ring("before", [P, TILES, H])
        cc = ring("cc", [P, TILES, H])
        vp = ring("vp", [P, TILES, H, W1E])
        ktok = ring("ktok", [P, TILES, D])
        A = ring("A", [P, H, C])
        S = ring("S", [P, 2, SV])
        den = ring("den", [P, H])
        rden = ring("rden", [P, H])
        on = ring("on", [P, D])
        oT = ring("oT", [P, D])
        sq = ring("sq", [P, D])
        o = ring("o", [P, TILES, D])
        ss = ring("ss", [P, TILES])
        ms = ring("ms", [P, TILES])
        rr = ring("rr", [P, TILES])
        tt = ring("tt", [P, TILES, D])
        h2 = ring("h2", [P, TILES, D])
        stat2 = ring("stat2", [P, TILES, 6])
        mv2 = ring("mv2", [P, TILES, 2])
        ve2 = ring("ve2", [P, 2, TILES])
        rn2 = ring("rn2", [P, 2, TILES])
        sc2 = ring("sc2", [P, TILES])
        y = ring("y", [P, TILES, D])

        bankX = ps("bankX", [P, 512])
        bankT = ps("bankT", [P, 512])
        bankV = ps("bankV", [P, 512])
        bankS = [ps("bankS0", [P, 512]), ps("bankS1", [P, 512])]
        state = ps("state", [P, 2, 512])
        bankO = ps("bankO", [P, 512])
        xT_ps = bankX[:, 0:GT]
        k_ps = bankX[:, 0:GT]
        q_ps = bankX[:, 0:GT]
        kt_ps = bankX[:, 0:GT]
        v_ps = bankV[:, 0:TILES * VD].rearrange("p (t n) -> p t n", t=TILES)
        cum_ps = bankV[:, TILES * VD:TILES * VD + TILES * H]
        nd_ps = bankO[:, 0:SV]
        oT_ps = bankT[:, 0:D]
        o_ps = bankT[:, D:2 * D]

        cst_in_sem, wts_sem, n_sem, rows_sem, pix_sem = (
            sem(n) for n in ("cst_loaded", "wts_loaded", "noisy_loaded", "rows_loaded", "pix_loaded"))
        s_zero = sem("zeroed")
        s_set = sem("set_dve")
        s_root = sem("rooted")
        s_noise = sem("noisy_ready")
        s_bias = sem("bias_parts")
        s_gps, s_ge, s_u, s_hps, s_himg, s_gd = (
            sem(n) for n in ("gate_product", "gate_exp", "u_ready", "himg_product", "himg_ready", "gate_dve"))
        s_hload = [sem(f"h_loaded{i}") for i in range(H_RING)]
        s_himgc = sem("himg_copied")
        s_stat = sem("stat_steps")
        s_ln = sem("ln_steps")
        s_xTps, s_xT, s_qps, s_kps, s_qer, s_ker, s_q, s_k = (
            sem(n) for n in ("xT_product", "xT_copied", "q_product", "k_product", "q_exp", "k_exp", "q_ready",
                             "k_ready"))
        s_qbd = [sem(f"q_blocks{g}") for g in range(GROUPS)]
        s_vps, s_ez, s_lam, s_L, s_before, s_cum, s_clip, s_dk, s_vp, s_ktps, s_kt = (
            sem(n) for n in ("v_product", "decay_exp", "lam_steps", "log_decay", "before_steps", "cum_product",
                             "clipped", "dk_ready", "vp_ready", "ktok_product", "ktok_copied"))
        s_sc, s_A, s_nd, s_on, s_st, s_S, s_oTps, s_oT, s_ops, s_osq = (
            sem(n) for n in ("scores_ready", "A_masked", "sums_ready", "norm_steps", "state_added", "state_copied",
                             "oT_product", "oT_copied", "o_product", "o_read"))
        s_ms, s_rr, s_t, s_h2, s_st2, s_rn2, s_y = (
            sem(n) for n in ("mean_square", "rms_inverse", "scaled", "h2_ready", "stat2_steps", "rn2_steps",
                             "y_ready"))
        s_out = [sem(f"stored{g}") for g in range(GROUPS)]

        text = txt.rearrange("b (c l) d -> b l c d", l=C)
        final = out.rearrange("b (c l) d -> b l c d", l=C)

        block = ctx.enter_context(nc.Block())

        def at(p, g):
            return p + g // GROUPS, g % GROUPS, GROUPS * p + g

        def over_steps(eng, step):
            step(0, 0, -2, True, False, False, False)
            step(0, 0, -1, True, True, False, False)
            for g in range(GROUPS):
                step(0, 0, g, True, True, True, g > 0)
            with eng.Fori(0, (PAIRS - 2) // 2) as turn:
                for i in range(2):
                    for g in range(GROUPS):
                        step(2 * turn + (1 + i), 1 - i, g, True, True, True, True)
            for g in range(GROUPS):
                step(PAIRS - 1, 1, g, g + 2 < GROUPS, g + 1 < GROUPS, True, True)
            step(PAIRS - 1, 1, GROUPS, False, False, False, True)

        def odd_at(odd, g):
            return (odd + g // GROUPS) % 2

        def h_slot(odd, g):
            return (GROUPS * odd + g) % H_RING

        def wait(eng, s, value):
            if not isinstance(value, int) or value > 0:
                eng.wait_ge(s, value)

        def wait_apart(eng, *waits):
            waits = [(s, v if isinstance(v, int) else eng.to_reg(v)) for s, v in waits]
            eng.wait_ge(cst_in_sem, 16)
            for s, v in waits:
                wait(eng, s, v)

        @block.sync
        def _(sp):
            sp.dma_start(rows[:], rows_in[0:1, :].broadcast_to([P, ROW_N])).then_inc(rows_sem, 16)
            sp.dma_start(cols[:], cols_in).then_inc(rows_sem, 16)
            sp.dma_start(w12[:], noisy_w).then_inc(n_sem, 16)
            sp.dma_start(sw12[:], noisy_sw).then_inc(n_sem, 16)
            sp.dma_start(pix[:], patches).then_inc(pix_sem, 16)
            sp.dma_start(wts[:], wts_in).then_inc(wts_sem, 16)
            sp.dma_start(cst[:], cst_in).then_inc(cst_in_sem, 16)

            def load(p, odd, g):
                pp, r, _ = at(p, g)
                slot = h_slot(odd, g)
                c0 = TILES * r
                j0 = 1 if r == 0 else 0
                for half in (0, 1):
                    sp.dma_start(h[slot][half * C:half * C + C, j0:TILES, :],
                                 text[2 * pp + half][:, c0 + j0 - 1:c0 + TILES - 1, :]).then_inc(s_hload[slot], 16)

            for g in range(GROUPS):
                load(0, 0, g)

            def step(p, odd, g, ahead, new, cur, old):
                if new:
                    pn, rn_, n = at(p, g + 1)
                    wait_apart(sp, (s_q, n + 1), (s_sc, TILES * (n - 2)))
                    if isinstance(n, int) and n < GROUPS:
                        sp.wait_ge(s_zero, 1)
                    for hd in range(H):
                        sp.dma_start(qbd[rn_][E * hd:E * hd + E, hd, :],
                                     q[rn_][E * hd:E * hd + E, :]).then_inc(s_qbd[rn_], 16)
                if cur and (ahead and not (isinstance(p, int) and p == PAIRS - 1)):
                    wait_apart(sp, (s_h2, at(p, g - 3)[2] + 1))
                    load(p, odd, g + 3)
                if old:
                    pm, r, m = at(p, g - 1)
                    wait_apart(sp, (s_y, m + 1))
                    for half in (0, 1):
                        sp.dma_start(final[2 * pm + half][:, TILES * r:TILES * r + TILES, :],
                                     y[r][half * C:half * C + C]).then_inc(s_out[r], 16)

            over_steps(sp, step)
            for r in range(GROUPS):
                sp.wait_ge(s_out[r], 32 * PAIRS)

        @block.tensor
        def _(pe):
            pe.wait_ge(s_noise, 1)
            pe.wait_ge(pix_sem, 16)
            for n in range(2):
                if n:
                    pe.wait_ge(s_u, 1)
                for layer, bank in ((0, bankX), (1, bankT)):
                    for kt in range(2):
                        mm = pe.matmul(bank[:, :], w12[:, 2 * layer + kt, :], pix[:, kt, 512 * n:512 * n + 512],
                                       start=(kt == 0), stop=(kt == 1))
                mm.then_inc(s_gps, 1)
            pe.wait_ge(s_bias, 1)
            pe.wait_ge(wts_sem, 16)
            for pr in range(PAIRS):
                if pr % 4 == 0:
                    pe.wait_ge(s_u, pr // 4 + 1)
                dst = bankS[pr // 4][:, P * (pr % 4):P * (pr % 4) + P]
                pe.matmul(dst, ones_b[:, :], bias_o[:, 1, :], start=True, stop=False)
                mm = pe.matmul(dst, u[:, pr // 4, P * (pr % 4):P * (pr % 4) + P], w_of["w3"], start=False, stop=True)
            mm.then_inc(s_hps, 1)
            pe.wait_ge(cst_in_sem, 16)

            def step(p, odd, g, ahead, new, cur, old):
                pn, nr, n = at(p, g + 1)
                pc, r, c = at(p, g)
                _, mr, m = at(p, g - 1)

                def scores(pair, c, r, j):
                    t = TILES * r + j
                    T = TILES * c + j
                    if j == 0:
                        pe.wait_ge(s_k, c + 1)
                        pe.wait_ge(s_qbd[r], 16 * H * (pair + 1))
                    wait(pe, s_A, T if t == 0 else T - 1)
                    for half in (0, 1):
                        x0 = P * j + C * half
                        mm = pe.matmul(bankS[t % 2][C * half:C * half + C, :], k[r][:, x0:x0 + C],
                                       qbd[r][:, :, x0:x0 + C], start=True, stop=True)
                    mm.then_inc(s_sc, 1)

                def turn(c, r, j):
                    T = TILES * c + j
                    pe.wait_ge(s_on, 3 * T + 3)
                    wait(pe, s_osq, T)
                    pe.transpose(oT_ps, on[j][:, :], cst_of["ident"]).then_inc(s_oTps, 1)

                def attend(c, r, j):
                    T = TILES * c + j
                    first = r == 0 and j == 0
                    if not first:
                        wait(pe, s_S, T)
                    wait_apart(pe, (s_A, T + 1), (s_on, 3 * T))
                    for half in (0, 1):
                        x0 = P * j + C * half
                        dst = nd_ps[C * half:C * half + C]
                        if not first:
                            pe.matmul(dst, q[r][:, x0:x0 + C], S[j][:, half, :], start=True, stop=False,
                                      skip_group_check=True)
                    for hd in range(H):
                        for half in (0, 1):
                            rows_ = slice(C * half, C * half + C)
                            mm = pe.matmul(nd_ps[rows_, W1E * hd:W1E * hd + W1E], A[j][rows_, hd, :],
                                           vp[r][rows_, j, hd, :], start=(first and hd == 0), stop=(hd == H - 1),
                                           skip_group_check=True)
                    mm.then_inc(s_nd, 1)

                def project(c, r, j):
                    T = TILES * c + j
                    pe.wait_ge(s_oT, T + 1)
                    pe.matmul(o_ps, ones_b[:, :], bias_o[:, 0, :], start=True, stop=False)
                    pe.matmul(o_ps, oT[j][:, :], w_of["wo"], start=False, stop=True).then_inc(s_ops, 1)

                def add_state(c, r, j):
                    T = TILES * c + j
                    if j == 0:
                        pe.wait_ge(s_kt, c + 1)
                        pe.wait_ge(s_vp, c + 1)
                    wait(pe, s_S, T)
                    for half in (0, 1):
                        rows_ = slice(C * half, C * half + C)
                        mm = pe.matmul(state[:, half, 0:SV], ktok[r][rows_, j, :], vp[r][rows_, j, :, :],
                                       start=(r == 0 and j == 0), stop=True, skip_group_check=True)
                    mm.then_inc(s_st, 1)

                if new:
                    pe.wait_ge(s_ln, 3 * n + 3)
                    wait(pe, s_kt, n)
                    for j in range(TILES):
                        mm = pe.transpose(xT_ps[:, P * j:P * j + P], xn[nr][:, j, :], cst_of["ident"])
                    mm.then_inc(s_xTps, 1)
                if cur:
                    scores(pc, c, r, 1)
                    add_state(c, r, 0)
                if old:
                    turn(m, mr, TILES - 1)
                if cur:
                    attend(c, r, 0)
                if old:
                    project(m, mr, TILES - 1)
                if new:
                    pe.wait_ge(s_xT, n + 1)
                    pe.matmul(q_ps, w_of["wq"], xT[nr][:, :], start=True, stop=True).then_inc(s_qps, 1)
                if cur:
                    scores(pc, c, r, 2)
                    add_state(c, r, 1)
                    turn(c, r, 0)
                if new:
                    wait(pe, s_vp, n)
                    pe.matmul(bankV[:, 0:TILES * VD], ones_b[:, :], bias_vd[:, :, :], start=True, stop=False,
                              skip_group_check=True)
                    for j in range(TILES):
                        mm = pe.matmul(v_ps[:, j, :], xT[nr][:, P * j:P * j + P], w_of["wvd"], start=False,
                                       stop=(j == TILES - 1), skip_group_check=True)
                    mm.then_inc(s_vps, 1)
                if cur:
                    attend(c, r, 1)
                    project(c, r, 0)
                if new:
                    pe.wait_ge(s_qer, n + 1)
                    pe.matmul(k_ps, w_of["wk"], xT[nr][:, :], start=True, stop=True).then_inc(s_kps, 1)
                if cur:
                    add_state(c, r, 2)
                    turn(c, r, 1)
                    attend(c, r, 2)
                if new:
                    pe.wait_ge(s_before, 3 * n + 3)
                    pe.matmul(cum_ps, cst_of["U"], L[nr][:, :, :], start=True, stop=False)
                    pe.matmul(cum_ps, cst_of["ones"], before[nr][:, :, :], start=False, stop=True).then_inc(s_cum, 1)
                if cur:
                    project(c, r, 1)
                if new:
                    pe.wait_ge(s_k, n + 1)
                    for j in range(TILES):
                        mm = pe.transpose(kt_ps[:, P * j:P * j + P], k[nr][:, P * j:P * j + P], cst_of["ident"])
                    mm.then_inc(s_ktps, 1)
                    scores(pn, n, nr, 0)

            over_steps(pe, step)

        @block.scalar
        def _(act):
            act.wait_ge(s_root, 1)
            act.activation(roots[:, :], roots[:, :], ACT.Sqrt)
            act.activation(rootn[:, :], rootn[:, :], ACT.Sqrt).then_inc(s_root, 1)
            act.preload_act_table_set("natural_log_exp_and_others")
            for n in range(2):
                act.wait_ge(s_gd, 7 * n + 2)
                act.activation(ge[:, :], ge[:, :], ACT.Exp).then_inc(s_ge, 1)

            def step(p, odd, g, ahead, new, cur, old):
                pn, nr, n = at(p, g + 1)
                pc, r, c = at(p, g)
                _, mr, m = at(p, g - 1)

                def copy_turned(c, j):
                    act.wait_ge(s_oTps, TILES * c + j + 1)
                    act.activation(oT[j][:, :], oT_ps, ACT.Copy).then_inc(s_oT, 1)

                def read_o(c, r, j):
                    act.wait_ge(s_ops, TILES * c + j + 1)
                    act.activation(o[r][:, j, :], o_ps, ACT.Copy)
                    act.activation(sq[j][:, :], o_ps, ACT.Square, accum_out=ss[r][:, j:j + 1]).then_inc(s_osq, 1)

                if new:
                    act.wait_ge(s_xTps, n + 1)
                    act.activation(xT[nr][:, :], xT_ps, ACT.Copy).then_inc(s_xT, 1)
                if old:
                    copy_turned(m, TILES - 1)
                    read_o(m, mr, TILES - 1)
                if new:
                    act.wait_ge(s_qps, n + 1)
                    act.activation(eq[nr][:, :], q_ps, ACT.Exp, bias=col["bq"])
                    act.activation(rq[nr][:, :], q_ps, ACT.Relu, bias=col["bq"]).then_inc(s_qer, 1)
                if cur:
                    copy_turned(c, 0)
                if new:
                    act.wait_ge(s_vps, n + 1)
                    act.activation(ez[nr][:, :, :], v_ps[:, :, D:VD], ACT.Exp, scale=-1.0).then_inc(s_ez, 1)
                if cur:
                    read_o(c, r, 0)
                if new:
                    act.wait_ge(s_kps, n + 1)
                    act.activation(ek[nr][:, :], k_ps, ACT.Exp, bias=col["bk"])
                    act.activation(rk[nr][:, :], k_ps, ACT.Relu, bias=col["bk"]).then_inc(s_ker, 1)
                    act.wait_ge(s_lam, 3 * n + 3)
                    act.activation(L[nr][:, :, :], lam[nr][:, :, :], ACT.Ln).then_inc(s_L, 1)
                if cur:
                    copy_turned(c, 1)
                if new:
                    act.wait_ge(s_clip, n + 1)
                    act.activation(vp[nr][:, :, :, E], cc[nr][:, :, :], ACT.Exp, scale=-1.0).then_inc(s_dk, 1)
                if cur:
                    read_o(c, r, 1)
                if new:
                    act.wait_ge(s_ktps, n + 1)
                    act.activation(ktok[nr][:, :, :], kt_ps.rearrange("p (t n) -> p t n", t=TILES),
                                   ACT.Copy).then_inc(s_kt, 1)

            over_steps(act, step)

        @block.vector
        def _(dve):
            dve.wait_ge(rows_sem, 32)
            steps = [0]

            def link(ins):
                steps[0] += 1
                ins.then_inc(s_set, 1)
                dve.wait_ge(s_set, steps[0])

            dve.tensor_copy(epsv[:, 0:1], col["eo1"])
            dve.tensor_copy(epsv[:, 1:2], col["eo2"])
            dve.tensor_copy(epsv[:, 2:6], cols[:, COL["ei1a"]:COL["ei1a"] + 4])
            link(dve.tensor_copy(epsv[:, 6:], rows[:, ROW["eo1"][0]:ROW["eo1"][0] + 2 * D]))
            dve.tensor_scalar(roots[:, :], epsv[:, :], 0.0, None, ALU.max)
            dve.tensor_scalar(rootn[:, :], epsv[:, :], -1.0, 0.0, ALU.mult, ALU.max).then_inc(s_root, 1)
            full = rows[:, 0:BR]
            link(dve.tensor_copy(part[0][:, :], full))
            link(dve.tensor_tensor(rest[0][:, :], full, part[0][:, :], ALU.subtract))
            link(dve.tensor_copy(part[1][:, :], rest[0][:, :]))
            link(dve.tensor_tensor(rest[1][:, :], rest[0][:, :], part[1][:, :], ALU.subtract))
            link(dve.tensor_copy(part[2][:, :], rest[1][:, :]))
            dve.memset(ones_b[:, :], 1.0)
            dve.memset(bias_vd[:, :, :], 0.0)
            link(dve.memset(bias_o[:, :, :], 0.0))
            for i in range(3):
                rw = slice(32 * i, 32 * i + 1)
                for j in range(TILES):
                    dve.tensor_copy(bias_vd[rw, j, :], part[i][rw, 0:VD])
                ins = dve.tensor_copy(bias_o[rw, :, :], part[i][rw, VD:BR].rearrange("p (t n) -> p t n", t=2))
            ins.then_inc(s_bias, 1)
            dve.wait_ge(s_root, 2)
            link(dve.tensor_tensor(noise[:, :], roots[:, :], rootn[:, :], ALU.subtract))
            dve.wait_ge(n_sem, 32)
            for layer in range(2):
                eo = noise[:, 6 + D * layer:6 + D * layer + D]
                for kt in range(2):
                    i = 2 * layer + kt
                    dve.scalar_tensor_tensor(nz12[:, i, :], eo, noise[:, 2 + i:3 + i], sw12[:, i, :], ALU.mult, ALU.mult)
                bias_cols = cols[:, COL["b1"] + 3 * layer:COL["b1"] + 3 * layer + 2]
                ins = dve.scalar_tensor_tensor(bias12[:, layer:layer + 1], noise[:, layer:layer + 1], bias_cols[:, 1:2],
                                               bias_cols[:, 0:1], ALU.mult, ALU.add)
            link(ins)
            dve.tensor_tensor(w12[:, :, :], w12[:, :, :], nz12[:, :, :], ALU.add).then_inc(s_noise, 1)
            for n in range(2):
                a = 7 * n
                dve.wait_ge(s_gps, n + 1)
                dve.tensor_scalar(gl[:, :], bankX[:, :], bias12[:, 0:1], None, ALU.add).then_inc(s_gd, 1)
                dve.wait_ge(s_gd, a + 1)
                dve.tensor_scalar(ge[:, :], gl[:, :], 20.0, None, ALU.min).then_inc(s_gd, 1)
                dve.wait_ge(s_ge, n + 1)
                dve.scalar_tensor_tensor(gn[:, :], ge[:, :], 2.0, ge[:, :], ALU.add, ALU.mult).then_inc(s_gd, 1)
                dve.wait_ge(s_gd, a + 3)
                dve.tensor_scalar(gr[:, :], gn[:, :], 2.0, None, ALU.add).then_inc(s_gd, 1)
                dve.wait_ge(s_gd, a + 4)
                dve.reciprocal(gm[:, :], gr[:, :]).then_inc(s_gd, 1)
                dve.wait_ge(s_gd, a + 5)
                dve.tensor_tensor(gn[:, :], gn[:, :], gm[:, :], ALU.mult).then_inc(s_gd, 1)
                dve.wait_ge(s_gd, a + 6)
                dve.tensor_tensor(gl[:, :], gl[:, :], gn[:, :], ALU.mult).then_inc(s_gd, 1)
                dve.wait_ge(s_gd, a + 7)
                dve.scalar_tensor_tensor(u[:, n, :], bankT[:, :], bias12[:, 1:2], gl[:, :], ALU.add,
                                         ALU.mult).then_inc(s_u, 1)
            dve.wait_ge(cst_in_sem, 16)
            dve.wait_ge(s_hps, 1)
            for pr in range(PAIRS):
                ins = dve.tensor_tensor(himg[:, pr, :], bankS[pr // 4][:, P * (pr % 4):P * (pr % 4) + P],
                                        cst_of["pos"], ALU.add)
            ins.then_inc(s_himg, 1)

            def step(p, odd, g, ahead, new, cur, old):
                pn, nr, n = at(p, g + 1)
                pc, r, c = at(p, g)
                _, mr, m = at(p, g - 1)

                def mask(c, r, j):
                    t = TILES * r + j
                    dve.wait_ge(s_sc, TILES * c + j + 1)
                    dve.tensor_tensor(A[j][:, :, :], bankS[t % 2][:, :].rearrange("p (h l) -> p h l", h=H),
                                      cst_of["mask"][:, None, :].broadcast_to([P, H, C]), ALU.mult).then_inc(s_A, 1)

                def norm(c, r, j):
                    T = TILES * c + j
                    nd = nd_ps.rearrange("p (h e) -> p h e", h=H)
                    dve.wait_ge(s_nd, T + 1)
                    dve.scalar_tensor_tensor(den[j][:, :], vp[r][:, j, :, E], DEN_EPS, nd[:, :, E], ALU.mult,
                                             ALU.add).then_inc(s_on, 1)
                    dve.wait_ge(s_on, 3 * T + 1)
                    dve.reciprocal(rden[j][:, :], den[j][:, :]).then_inc(s_on, 1)
                    dve.wait_ge(s_on, 3 * T + 2)
                    dve.tensor_tensor(on[j][:, :].rearrange("p (h e) -> p h e", h=H), nd[:, :, 0:E],
                                      rden[j][:, :, None].broadcast_to([P, H, E]), ALU.mult).then_inc(s_on, 1)

                def copy_state(c, r, j):
                    dve.wait_ge(s_st, TILES * c + j + 1)
                    dve.tensor_tensor(S[(j + 1) % TILES][:, :, :], state[:, :, 0:SV],
                                      cst_of["blocks"][:, None, :].broadcast_to([P, 2, SV]), ALU.mult).then_inc(s_S, 1)

                def statistics(stat, mv, ve, s, n, src, eps):
                    for j in range(TILES):
                        ins = dve.bn_stats(stat[:, j, :], src[:, j, :])
                    ins.then_inc(s, 1)
                    wait_apart(dve, (s, 3 * n + 1))
                    for j in range(TILES):
                        ins = dve.bn_aggr(mv[:, j, :], stat[:, j, :])
                    ins.then_inc(s, 1)
                    dve.wait_ge(s, 3 * n + 2)
                    dve.tensor_scalar(ve[:, 0, :], mv[:, :, 1], eps, None, ALU.add)
                    dve.tensor_scalar(ve[:, 1, :], mv[:, :, 0], -1.0, None, ALU.mult).then_inc(s, 1)

                if cur:
                    mask(c, r, 1)
                    copy_state(c, r, 0)
                if ahead:
                    pa, ar, a = at(p, g + 2)
                    ah = h_slot(odd, g + 2)
                    dve.wait_ge(s_hload[ah], 16 * (pa - odd_at(odd, g + 2)) + 32)
                    if ar == 0:
                        dve.wait_ge(s_himgc, pa + 1)
                    statistics(stat[ar], mv[ar], ve[ar], s_stat, a, h[ah], LN_EPS)
                if cur:
                    norm(c, r, 0)
                if new:
                    dve.wait_ge(s_qer, n + 1)
                    dve.scalar_tensor_tensor(q[nr][:, :], eq[nr][:, :], 1.0, rq[nr][:, :], ALU.min,
                                             ALU.add).then_inc(s_q, 1)
                if cur:
                    mask(c, r, 2)
                if old:
                    dve.wait_ge(s_osq, TILES * (m + 1))
                    dve.tensor_scalar(ms[mr][:, :], ss[mr][:, :], 1.0 / D, RMS_EPS, ALU.mult, ALU.add).then_inc(s_ms, 1)
                if cur:
                    copy_state(c, r, 1)
                if old:
                    dve.wait_ge(s_rr, m + 1)
                    for j in range(TILES):
                        ins = dve.scalar_tensor_tensor(tt[mr][:, j, :], o[mr][:, j, :], rr[mr][:, j:j + 1],
                                                       row_of["ns"], ALU.mult, ALU.mult)
                    ins.then_inc(s_t, 1)
                if new:
                    dve.wait_ge(s_ez, n + 1)
                    dve.tensor_scalar(eu[nr][:, :, :], ez[nr][:, :, :], 1.0, None, ALU.add).then_inc(s_lam, 1)
                    dve.wait_ge(s_lam, 3 * n + 1)
                    dve.reciprocal(er[nr][:, :, :], eu[nr][:, :, :]).then_inc(s_lam, 1)
                    dve.wait_ge(s_lam, 3 * n + 2)
                    dve.tensor_scalar(lam[nr][:, :, :], er[nr][:, :, :], 0.1, 0.9, ALU.mult, ALU.add).then_inc(s_lam, 1)
                if cur:
                    norm(c, r, 1)
                    copy_state(c, r, 2)
                if new:
                    dve.wait_ge(s_ker, n + 1)
                    dve.scalar_tensor_tensor(k[nr][:, :], ek[nr][:, :], 1.0, rk[nr][:, :], ALU.min,
                                             ALU.add).then_inc(s_k, 1)
                    dve.wait_ge(s_L, n + 1)
                    if nr == 0:
                        dve.memset(before[nr][:, 0, :], 0.0).then_inc(s_before, 1)
                    else:
                        dve.tensor_tensor(before[nr][:, 0, :], before[nr - 1][:, TILES - 1, :], L[nr - 1][:, TILES - 1, :],
                                          ALU.add).then_inc(s_before, 1)
                    for j in range(1, TILES):
                        dve.wait_ge(s_before, 3 * n + j)
                        dve.tensor_tensor(before[nr][:, j, :], before[nr][:, j - 1, :], L[nr][:, j - 1, :],
                                          ALU.add).then_inc(s_before, 1)
                if cur:
                    norm(c, r, 2)
                if new:
                    dve.wait_ge(s_cum, n + 1)
                    dve.tensor_scalar(cc[nr][:, :, :], cum_ps.rearrange("p (t h) -> p t h", t=TILES), -50.0, 50.0,
                                      ALU.max, ALU.min).then_inc(s_clip, 1)
                    dve.wait_ge(s_dk, n + 1)
                    for j in range(TILES):
                        ins = dve.tensor_tensor(vp[nr][:, j, :, 0:E], v_ps[:, j, 0:D].rearrange("p (h e) -> p h e", h=H),
                                                vp[nr][:, j, :, E:W1E].broadcast_to([P, H, E]), ALU.mult)
                    ins.then_inc(s_vp, 1)
                    mask(n, nr, 0)
                if old:
                    dve.wait_ge(s_h2, m + 1)
                    statistics(stat2[mr], mv2[mr], ve2[mr], s_st2, m, h2[mr], LN_EPS)

            over_steps(dve, step)

        @block.gpsimd
        def _(pool):
            for r in range(GROUPS):
                ins = pool.memset(qbd[r][:, :, :], 0.0)
            ins.then_inc(s_zero, 1)
            pool.memset(minus_half[:, :], -0.5).then_inc(s_zero, 1)
            pool.wait_ge(s_zero, 2)
            pool.wait_ge(s_himg, 1)

            def copy_image(pair, slot):
                pool.tensor_copy(h[slot][:, 0:1, :], himg[:, bass.ds(pair, 1), :]).then_inc(s_himgc, 1)

            copy_image(0, 0)

            def step(p, odd, g, ahead, new, cur, old):
                pa, ar, a = at(p, g + 2)
                ah = h_slot(odd, g + 2)
                pm, mr, m = at(p, g - 1)
                mh = h_slot(odd, g - 1)
                if ahead:
                    pool.wait_ge(s_stat, 3 * a + 3)
                    pool.tensor_tensor(rn[ar][:, 0, :], ve[ar][:, 0, :], minus_half[:, :], ALU.pow).then_inc(s_ln, 1)
                    pool.wait_ge(s_ln, 3 * a + 1)
                    pool.tensor_tensor(rn[ar][:, 1, :], ve[ar][:, 1, :], rn[ar][:, 0, :], ALU.mult).then_inc(s_ln, 1)
                    wait_apart(pool, (s_ln, 3 * a + 2))
                    for j in range(TILES):
                        ins = pool.tensor_scalar(xn[ar][:, j, :], h[ah][:, j, :], rn[ar][:, 0, j:j + 1],
                                                 rn[ar][:, 1, j:j + 1], ALU.mult, ALU.add)
                    ins.then_inc(s_ln, 1)
                if old:
                    pool.wait_ge(s_ms, m + 1)
                    pool.tensor_tensor(rr[mr][:, :], ms[mr][:, :], minus_half[:, :], ALU.pow).then_inc(s_rr, 1)
                    pool.wait_ge(s_t, m + 1)
                    pool.tensor_tensor(h2[mr][:, :, :], h[mh][:, :, :], tt[mr][:, :, :], ALU.add).then_inc(s_h2, 1)
                if cur and g == 0 and not (isinstance(p, int) and p == PAIRS - 1):
                    wait(pool, s_h2, at(p, GROUPS - H_RING)[2] + 1)
                    copy_image(p + 1, h_slot(odd, GROUPS))
                if old:
                    pool.wait_ge(s_st2, 3 * m + 3)
                    pool.tensor_tensor(rn2[mr][:, 0, :], ve2[mr][:, 0, :], minus_half[:, :], ALU.pow).then_inc(s_rn2, 1)
                    pool.wait_ge(s_rn2, 3 * m + 1)
                    pool.tensor_tensor(rn2[mr][:, 1, :], ve2[mr][:, 1, :], rn2[mr][:, 0, :], ALU.mult).then_inc(s_rn2, 1)
                    pool.tensor_scalar(sc2[mr][:, :], rn2[mr][:, 0, :], 1.0, None, ALU.add).then_inc(s_rn2, 1)
                if old:
                    wait_apart(pool, (s_rn2, 3 * m + 3), (s_out[mr], 32 * pm))
                    for j in range(TILES):
                        ins = pool.tensor_scalar(y[mr][:, j, :], h2[mr][:, j, :], sc2[mr][:, j:j + 1],
                                                 rn2[mr][:, 1, j:j + 1], ALU.mult, ALU.add)
                    ins.then_inc(s_y, 1)

            over_steps(pool, step)
    return nc


def _constants():
    s = np.arange(P)
    same = (s[:, None] // C) == (s[None, :] // C)
    U = (same & (s[:, None] <= s[None, :])).astype(np.float32)
    ones = same.astype(np.float32)
    ident = np.eye(P, dtype=np.float32)
    mask = ((s[:, None] % C) <= np.arange(C)[None, :]).astype(np.float32)
    blocks = ((s[:, None] // E) == (np.arange(SV)[None, :] // W1E)).astype(np.float32)
    div = np.exp(np.arange(0, D, 2, dtype=np.float32) * np.float32(-np.log(10000.0) / D)).astype(np.float32)
    ang = np.arange(C, dtype=np.float32)[:, None] * div
    pos = np.stack([np.sin(ang), np.cos(ang)], axis=-1).reshape(C, D).astype(np.float32)
    return np.concatenate([U, ones, ident, mask, blocks, np.concatenate([pos, pos])], axis=1)


def kernel(**inputs):
    import concourse.bacc as _bacc
    from concourse.bass_utils import run_bass_kernel_spmd as _run

    a = {n: np.asarray(v) for n, v in inputs.items()}
    w = lambda n: a["L0_" + n]
    x = a["x"].reshape(BATCHES, 8, 16, 8, 16).transpose(2, 4, 0, 1, 3).reshape(2, P, BATCHES * C).transpose(1, 0, 2)
    qkv = w("attn_qkv_w")
    wts = np.concatenate([qkv[0:D].T, qkv[D:2 * D].T, qkv[2 * D:3 * D].T, w("attn_decay_w").T, w("attn_out_w").T,
                          w("tok_W3_w").T], axis=1)
    by_pixel = lambda m: m.T.reshape(2, P, D).transpose(1, 0, 2)
    noisy_w = np.concatenate([by_pixel(w("tok_W1_w")), by_pixel(w("tok_W2_w"))], axis=1)
    noisy_sw = np.concatenate([by_pixel(w("tok_W1_sw")), by_pixel(w("tok_W2_sw"))], axis=1)
    qkv_b = w("attn_qkv_b")
    cols = np.stack([qkv_b[0:D], qkv_b[D:2 * D], w("tok_W1_b"), w("tok_W1_sb"), w("tok_eps_out1"), w("tok_W2_b"),
                     w("tok_W2_sb"), w("tok_eps_out2"), w("tok_eps_in1")[0:P], w("tok_eps_in1")[P:],
                     w("tok_eps_in2")[0:P], w("tok_eps_in2")[P:]], axis=1)
    rows = np.concatenate([qkv_b[2 * D:3 * D], w("attn_decay_b"), w("attn_out_b"), w("tok_W3_b"),
                           w("attn_norm_scale"), w("tok_eps_out1"), w("tok_eps_out2")])[None, :]
    arrays = {"txt": a["txt"], "patches": x, "constants": _constants(), "weights": wts, "noisy_w": noisy_w,
              "noisy_sw": noisy_sw, "columns": cols, "rows": rows}
    nc = _bacc.Bacc("TRN2", target_bir_lowering=False, num_devices=1)
    args = []
    for name in arrays:
        arrays[name] = np.ascontiguousarray(arrays[name])
        args.append(nc.dram_tensor(f"in_{name}", arrays[name].shape, mybir.dt.from_np(arrays[name].dtype),
                                   kind="ExternalInput").ap())
    args.append(nc.dram_tensor("result", (BATCHES, C + TEXT, D), F32, kind="ExternalOutput").ap())
    build(nc, *args)
    r = _run(nc, [{f"in_{n}": v for n, v in arrays.items()}], core_ids=[0])
    return r.results[0]["result"]
```

```python
from contextlib import ExitStack

import numpy as np

import concourse.bass as bass
from concourse import mybir

F32 = mybir.dt.float32
BF16 = mybir.dt.bfloat16
ALU = mybir.AluOpType
ACT = mybir.ActivationFunctionType

P = 128
BATCHES = 16
PAIRS = BATCHES // 2
D = 128
H = 8
E = D // H
C = 64
TEXT = 512
CHUNKS = (C + TEXT) // C
TILES = 3
GROUPS = CHUNKS // TILES
GT = TILES * P
VD = D + H
W1E = E + 1
SV = H * W1E
SB = SV // 2
KEEP = 8
H_RING = 2 * GROUPS
PIX = 256
LN_EPS = 1e-5
RMS_EPS = 1e-8
DEN_EPS = 1e-6 * E ** 0.5

CST = {"U": (0, P), "ones": (P, P), "ident": (2 * P, P), "mask": (3 * P, C), "blocks": (3 * P + C, SV),
       "pos": (3 * P + C + SV, P)}
CST_N = 3 * P + C + SV + P
WTS = {"wq": (0, D), "wk": (D, D), "wvd": (2 * D, VD), "wo": (2 * D + VD, D), "w3": (3 * D + VD, D)}
WTS_N = 4 * D + VD
COL = {n: i for i, n in enumerate(["bq", "bk", "b1", "sb1", "eo1", "b2", "sb2", "eo2",
                                   "ei1a", "ei1b", "ei2a", "ei2b"])}
ROW = {"vd": (0, VD), "o": (VD, D), "w3": (VD + D, D), "ns": (VD + 2 * D, D), "eo1": (VD + 3 * D, D),
       "eo2": (VD + 4 * D, D)}
ROW_N = VD + 5 * D


def build(nc, txt, patches, cst_in, wts_in, noisy_w, noisy_sw, cols_in, rows_in, out):
    with ExitStack() as ctx:
        def sb(name, shape, dt=F32):
            return ctx.enter_context(nc.sbuf_tensor(name, shape, dt))

        def ps(name, shape):
            return ctx.enter_context(nc.psum_tensor(name, shape, F32))

        def sem(name):
            return ctx.enter_context(nc.semaphore(name))

        cst = sb("cst", [P, CST_N])
        wts = sb("wts", [P, WTS_N])
        w12 = sb("w12", [P, 4, D])
        sw12 = sb("sw12", [P, 4, D])
        nz12 = sb("nz12", [P, 4, D])
        cols = sb("cols", [P, len(COL)])
        rows = sb("rows", [P, ROW_N])
        pix = sb("pix", [P, 2, BATCHES * C])
        cst_of = {n: cst[:, a:a + w] for n, (a, w) in CST.items()}
        w_of = {n: wts[:, a:a + w] for n, (a, w) in WTS.items()}
        row_of = {n: rows[:, a:a + w] for n, (a, w) in ROW.items()}
        col = {n: cols[:, i:i + 1] for n, i in COL.items()}
        roots = sb("roots", [P, 6 + 2 * D])
        rootn = sb("rootn", [P, 6 + 2 * D])
        noise = sb("noise", [P, 6 + 2 * D])
        epsv = sb("epsv", [P, 6 + 2 * D])
        bias12 = sb("bias12", [P, 2])
        minus_half = sb("minus_half", [P, TILES])
        ones_b = sb("ones_b", [P, P], BF16)
        BR = VD + 2 * D
        part = [sb(f"part{i}", [P, BR], BF16) for i in range(3)]
        rest = [sb(f"rest{i}", [P, BR]) for i in range(2)]
        bias_vd = sb("bias_vd", [P, TILES, VD], BF16)
        bias_o = sb("bias_o", [P, 2, D], BF16)
        gate = sb("gate", [P, P])
        inner = sb("inner", [P, P])
        clamped = sb("clamped", [P, P])
        expg = sb("expg", [P, P])
        num = sb("num", [P, P])
        below = sb("below", [P, P])
        inv = sb("inv", [P, P])
        ratio = sb("ratio", [P, P])
        gated = sb("gated", [P, P])
        u = sb("u", [P, P])

        def ring(name, shape, dt=F32):
            return [sb(f"{name}{g}", shape, dt) for g in range(GROUPS)]

        h = [sb(f"h{i}", [P, TILES, D]) for i in range(H_RING)]
        stat = ring("stat", [P, TILES, 6])
        mv = ring("mv", [P, TILES, 2])
        ve = ring("ve", [P, 2, TILES])
        rn = ring("rn", [P, 2, TILES])
        xn = ring("xn", [P, TILES, D])
        xT = ring("xT", [P, GT])
        eq = ring("eq", [P, GT])
        rq = ring("rq", [P, GT])
        ek = ring("ek", [P, GT])
        rk = ring("rk", [P, GT])
        q = ring("q", [P, GT])
        k = ring("k", [P, GT])
        qbd = ring("qbd", [P, H, GT])
        ez = ring("ez", [P, TILES, H])
        eu = ring("eu", [P, TILES, H])
        er = ring("er", [P, TILES, H])
        lam = ring("lam", [P, TILES, H])
        L = ring("L", [P, TILES, H])
        before = ring("before", [P, TILES, H])
        cc = ring("cc", [P, TILES, H])
        vp = ring("vp", [P, TILES, H, W1E])
        ktok = ring("ktok", [P, TILES, D])
        A = ring("A", [P, H, C])
        S = ring("S", [P, 2, SV])
        den = ring("den", [P, H])
        rden = ring("rden", [P, H])
        on = ring("on", [P, D])
        oT = ring("oT", [P, D])
        sq = ring("sq", [P, D])
        o = ring("o", [P, TILES, D])
        ss = ring("ss", [P, TILES])
        ms = ring("ms", [P, TILES])
        rr = ring("rr", [P, TILES])
        tt = ring("tt", [P, TILES, D])
        h2 = ring("h2", [P, TILES, D])
        stat2 = ring("stat2", [P, TILES, 6])
        mv2 = ring("mv2", [P, TILES, 2])
        ve2 = ring("ve2", [P, 2, TILES])
        rn2 = ring("rn2", [P, 2, TILES])
        sc2 = ring("sc2", [P, TILES])
        y = ring("y", [P, TILES, D])

        bankX = ps("bankX", [P, 512])
        bankT = ps("bankT", [P, 512])
        bankV = ps("bankV", [P, 512])
        bankS = [ps("bankS0", [P, 512]), ps("bankS1", [P, 512])]
        state = ps("state", [P, 2, 512])
        bankO = ps("bankO", [P, 512])
        xT_ps = bankX[:, 0:GT]
        k_ps = bankX[:, 0:GT]
        q_ps = bankX[:, 0:GT]
        kt_ps = bankX[:, 0:GT]
        v_ps = bankV[:, 0:TILES * VD].rearrange("p (t n) -> p t n", t=TILES)
        cum_ps = bankV[:, TILES * VD:TILES * VD + TILES * H]
        nd_ps = bankO[:, 0:SV]
        oT_ps = bankT[:, 0:D]
        o_ps = bankT[:, D:2 * D]
        gate_ps = bankT[:, 0:P]
        inner_ps = bankT[:, P:2 * P]
        himg_ps = bankT[:, 0:P]

        cst_in_sem, wts_sem, n_sem, rows_sem, pix_sem = (
            sem(n) for n in ("cst_loaded", "wts_loaded", "noisy_loaded", "rows_loaded", "pix_loaded"))
        s_zero = sem("zeroed")
        s_set = sem("set_dve")
        s_root = sem("rooted")
        s_noise = sem("noisy_ready")
        s_blank = sem("bias_blank")
        s_parts = sem("parts_steps")
        s_bias = sem("bias_parts")
        s_gps, s_ge, s_hps, s_himg, s_gd = (
            sem(n) for n in ("gate_product", "gate_exp", "himg_product", "himg_ready", "gate_steps"))
        s_hload = [sem(f"h_loaded{i}") for i in range(H_RING)]
        s_stat = sem("stat_steps")
        s_ln = sem("ln_steps")
        s_xTps, s_xT, s_qps, s_kps, s_qer, s_ker, s_q, s_k = (
            sem(n) for n in ("xT_product", "xT_copied", "q_product", "k_product", "q_exp", "k_exp", "q_ready",
                             "k_ready"))
        s_qbd = [sem(f"q_blocks{g}") for g in range(GROUPS)]
        s_vps, s_ez, s_lam, s_L, s_before, s_cum, s_clip, s_dk, s_vp, s_ktps, s_kt = (
            sem(n) for n in ("v_product", "decay_exp", "lam_steps", "log_decay", "before_steps", "cum_product",
                             "clipped", "dk_ready", "vp_ready", "ktok_product", "ktok_copied"))
        s_sc, s_A, s_nd, s_on, s_st, s_S, s_oTps, s_oT, s_ops, s_osq = (
            sem(n) for n in ("scores_ready", "A_masked", "sums_ready", "norm_steps", "state_added", "state_copied",
                             "oT_product", "oT_copied", "o_product", "o_read"))
        s_ms, s_rr, s_t, s_h2, s_st2, s_rn2, s_y = (
            sem(n) for n in ("mean_square", "rms_inverse", "scaled", "h2_ready", "stat2_steps", "rn2_steps",
                             "y_ready"))
        s_out = [sem(f"stored{g}") for g in range(GROUPS)]

        text = txt.rearrange("b (c l) d -> b l c d", l=C)
        final = out.rearrange("b (c l) d -> b l c d", l=C)

        block = ctx.enter_context(nc.Block())

        def at(p, g):
            return p + g // GROUPS, g % GROUPS, GROUPS * p + g

        def over_steps(eng, step):
            step(0, 0, -2, True, False, False, False)
            step(0, 0, -1, True, True, False, False)
            for g in range(GROUPS):
                step(0, 0, g, True, True, True, g > 0)
            with eng.Fori(0, (PAIRS - 4) // 2) as turn:
                for i in range(2):
                    for g in range(GROUPS):
                        step(2 * turn + (1 + i), 1 - i, g, True, True, True, True)
            for p in (PAIRS - 3, PAIRS - 2):
                for g in range(GROUPS):
                    step(p, p % 2, g, True, True, True, True)
            for g in range(GROUPS):
                step(PAIRS - 1, 1, g, g + 2 < GROUPS, g + 1 < GROUPS, True, True)
            step(PAIRS - 1, 1, GROUPS, False, False, False, True)

        def odd_at(odd, g):
            return (odd + g // GROUPS) % 2

        GATE = 9

        def h_slot(odd, g):
            return (GROUPS * odd + g) % H_RING

        def gate_here(p, g):
            return (g == -1) or (g == GROUPS - 1 and not (isinstance(p, int) and p >= PAIRS - 2))

        def gate_turn(p, g):
            return 1 if g == -1 else p + 2

        def h_here(p):
            return not (isinstance(p, int) and p == PAIRS - 1)

        def wait(eng, s, value):
            if not isinstance(value, int) or value > 0:
                eng.wait_ge(s, value)

        def wait_apart(eng, *waits):
            waits = [(s, v if isinstance(v, int) else eng.to_reg(v)) for s, v in waits]
            eng.wait_ge(cst_in_sem, 16)
            for s, v in waits:
                wait(eng, s, v)

        @block.sync
        def _(sp):
            sp.dma_start(rows[:], rows_in[0:1, :].broadcast_to([P, ROW_N])).then_inc(rows_sem, 16)
            sp.dma_start(cols[:], cols_in).then_inc(rows_sem, 16)
            sp.dma_start(w12[:], noisy_w).then_inc(n_sem, 16)
            sp.dma_start(sw12[:], noisy_sw).then_inc(n_sem, 16)
            sp.dma_start(pix[:], patches).then_inc(pix_sem, 16)
            sp.dma_start(wts[:], wts_in).then_inc(wts_sem, 16)
            sp.dma_start(cst[:], cst_in).then_inc(cst_in_sem, 16)

            def load(p, odd, g):
                pp, r, _ = at(p, g)
                slot = h_slot(odd, g)
                c0 = TILES * r
                j0 = 1 if r == 0 else 0
                for half in (0, 1):
                    sp.dma_start(h[slot][half * C:half * C + C, j0:TILES, :],
                                 text[2 * pp + half][:, c0 + j0 - 1:c0 + TILES - 1, :]).then_inc(s_hload[slot], 16)

            for g in range(GROUPS):
                load(0, 0, g)

            def step(p, odd, g, ahead, new, cur, old):
                if new:
                    pn, rn_, n = at(p, g + 1)
                    wait_apart(sp, (s_q, n + 1), (s_sc, TILES * (n - 2)))
                    if isinstance(n, int) and n < GROUPS:
                        sp.wait_ge(s_zero, 1)
                    for hd in range(H):
                        sp.dma_start(qbd[rn_][E * hd:E * hd + E, hd, :],
                                     q[rn_][E * hd:E * hd + E, :]).then_inc(s_qbd[rn_], 16)
                if cur and (ahead and not (isinstance(p, int) and p == PAIRS - 1)):
                    wait_apart(sp, (s_h2, at(p, g - 3)[2] + 1))
                    load(p, odd, g + 3)
                if old:
                    pm, r, m = at(p, g - 1)
                    wait_apart(sp, (s_y, m + 1))
                    for half in (0, 1):
                        sp.dma_start(final[2 * pm + half][:, TILES * r:TILES * r + TILES, :],
                                     y[r][half * C:half * C + C]).then_inc(s_out[r], 16)

            over_steps(sp, step)
            for r in range(GROUPS):
                sp.wait_ge(s_out[r], 32 * PAIRS)

        @block.tensor
        def _(pe):
            def image_gate(x0, n):
                for dst, layer in ((gate_ps, 0), (inner_ps, 1)):
                    for kt in range(2):
                        mm = pe.matmul(dst[:, 0:n], w12[:, 2 * layer + kt, :], x0(kt), start=(kt == 0), stop=(kt == 1))
                mm.then_inc(s_gps, 1)

            def image_h(turn, n):
                pe.wait_ge(s_gd, GATE * turn + GATE)
                for x0 in range(0, n, P):
                    pe.matmul(himg_ps[:, x0:x0 + P], ones_b[:, :], bias_o[:, 1, :], start=True, stop=False)
                    mm = pe.matmul(himg_ps[:, x0:x0 + P], u[:, x0:x0 + P], w_of["w3"], start=False, stop=True)
                mm.then_inc(s_hps, 1)

            pe.wait_ge(s_noise, 1)
            pe.wait_ge(pix_sem, 16)
            image_gate(lambda kt: pix[:, kt, 0:P], P)
            pe.wait_ge(s_bias, 1)
            pe.wait_ge(wts_sem, 16)
            image_h(0, P)
            pe.wait_ge(s_bias, 2)
            pe.wait_ge(cst_in_sem, 16)

            def step(p, odd, g, ahead, new, cur, old):
                pn, nr, n = at(p, g + 1)
                pc, r, c = at(p, g)
                _, mr, m = at(p, g - 1)

                def scores(pair, c, r, j):
                    t = TILES * r + j
                    T = TILES * c + j
                    if j == 0:
                        pe.wait_ge(s_k, c + 1)
                        pe.wait_ge(s_qbd[r], 16 * H * (pair + 1))
                    wait(pe, s_A, T if t == 0 else T - 1)
                    for half in (0, 1):
                        x0 = P * j + C * half
                        mm = pe.matmul(bankS[t % 2][C * half:C * half + C, :], k[r][:, x0:x0 + C],
                                       qbd[r][:, :, x0:x0 + C], start=True, stop=True)
                    mm.then_inc(s_sc, 1)

                def turn(c, r, j):
                    T = TILES * c + j
                    pe.wait_ge(s_on, 3 * T + 3)
                    wait(pe, s_osq, T)
                    pe.transpose(oT_ps, on[j][:, :], cst_of["ident"]).then_inc(s_oTps, 1)

                def attend(c, r, j):
                    T = TILES * c + j
                    first = r == 0 and j == 0
                    if not first:
                        wait(pe, s_S, T)
                    wait_apart(pe, (s_A, T + 1), (s_on, 3 * T))
                    for half in (0, 1):
                        x0 = P * j + C * half
                        dst = nd_ps[C * half:C * half + C]
                        if not first:
                            pe.matmul(dst, q[r][:, x0:x0 + C], S[j][:, half, :], start=True, stop=False,
                                      skip_group_check=True)
                    for hd in range(H):
                        for half in (0, 1):
                            rows_ = slice(C * half, C * half + C)
                            mm = pe.matmul(nd_ps[rows_, W1E * hd:W1E * hd + W1E], A[j][rows_, hd, :],
                                           vp[r][rows_, j, hd, :], start=(first and hd == 0), stop=(hd == H - 1),
                                           skip_group_check=True)
                    mm.then_inc(s_nd, 1)

                def project(c, r, j):
                    T = TILES * c + j
                    pe.wait_ge(s_oT, T + 1)
                    pe.matmul(o_ps, ones_b[:, :], bias_o[:, 0, :], start=True, stop=False)
                    pe.matmul(o_ps, oT[j][:, :], w_of["wo"], start=False, stop=True).then_inc(s_ops, 1)

                def keep_clock(count):
                    for _ in range(count):
                        pe.matmul(bankX[:, 0:TILES * VD], ones_b[:, :], bias_vd[:, :, :], start=True, stop=True)

                def add_state(c, r, j):
                    T = TILES * c + j
                    wait_apart(pe, *(((s_kt, c + 1), (s_vp, c + 1)) if j == 0 else ()), (s_S, T))
                    for half in (0, 1):
                        rows_ = slice(C * half, C * half + C)
                        for hh in (0, 1):
                            mm = pe.matmul(state[C * hh:C * hh + C, half, 0:SB], ktok[r][rows_, j, C * hh:C * hh + C],
                                           vp[r][rows_, j, H // 2 * hh:H // 2 * hh + H // 2, :],
                                           start=(r == 0 and j == 0), stop=True, skip_group_check=True)
                    mm.then_inc(s_st, 1)

                if new:
                    pe.wait_ge(s_ln, 3 * n + 3)
                    wait(pe, s_kt, n)
                    for j in range(TILES):
                        mm = pe.transpose(xT_ps[:, P * j:P * j + P], xn[nr][:, j, :], cst_of["ident"])
                    mm.then_inc(s_xTps, 1)
                if cur:
                    scores(pc, c, r, 1)
                    add_state(c, r, 0)
                if new:
                    pe.wait_ge(s_xT, n + 1)
                    pe.matmul(q_ps, w_of["wq"], xT[nr][:, :], start=True, stop=True).then_inc(s_qps, 1)
                if old:
                    turn(m, mr, TILES - 1)
                if cur:
                    attend(c, r, 0)
                if old:
                    project(m, mr, TILES - 1)
                if new:
                    pe.wait_ge(s_qer, n + 1)
                    pe.matmul(k_ps, w_of["wk"], xT[nr][:, :], start=True, stop=True).then_inc(s_kps, 1)
                if cur:
                    scores(pc, c, r, 2)
                    add_state(c, r, 1)
                    turn(c, r, 0)
                if new:
                    wait(pe, s_vp, n)
                    pe.matmul(bankV[:, 0:TILES * VD], ones_b[:, :], bias_vd[:, :, :], start=True, stop=False,
                              skip_group_check=True)
                    for j in range(TILES):
                        mm = pe.matmul(v_ps[:, j, :], xT[nr][:, P * j:P * j + P], w_of["wvd"], start=False,
                                       stop=(j == TILES - 1), skip_group_check=True)
                    mm.then_inc(s_vps, 1)
                if cur:
                    attend(c, r, 1)
                    project(c, r, 0)
                if cur:
                    add_state(c, r, 2)
                if new:
                    pe.wait_ge(s_ker, n + 1)
                    keep_clock(KEEP)
                if cur:
                    if gate_here(p, g):
                        pe.wait_ge(s_osq, TILES * c + 1)
                        image_gate(lambda kt: pix[:, kt, bass.ds(P * (p + 2), P)], P)
                    elif g == 0 and h_here(p):
                        pe.wait_ge(s_osq, TILES * c + 1)
                        image_h(p + 1, P)
                    else:
                        turn(c, r, 1)
                    attend(c, r, 2)
                    if gate_here(p, g):
                        pe.wait_ge(s_gd, GATE * (p + 2) + 2)
                        turn(c, r, 1)
                    elif g == 0 and h_here(p):
                        keep_clock(2)
                        pe.wait_ge(s_himg, p + 2)
                        turn(c, r, 1)
                if g == -1:
                    pe.wait_ge(s_himg, 1)
                    image_gate(lambda kt: pix[:, kt, P:2 * P], P)
                if new:
                    pe.wait_ge(s_before, 3 * n + 3)
                    pe.matmul(cum_ps, cst_of["U"], L[nr][:, :, :], start=True, stop=False)
                    pe.matmul(cum_ps, cst_of["ones"], before[nr][:, :, :], start=False, stop=True).then_inc(s_cum, 1)
                if cur:
                    project(c, r, 1)
                if new:
                    pe.wait_ge(s_k, n + 1)
                    for j in range(TILES):
                        mm = pe.transpose(kt_ps[:, P * j:P * j + P], k[nr][:, P * j:P * j + P], cst_of["ident"])
                    mm.then_inc(s_ktps, 1)
                    scores(pn, n, nr, 0)

            over_steps(pe, step)

        @block.scalar
        def _(act):
            act.wait_ge(s_root, 1)
            act.activation(roots[:, :], roots[:, :], ACT.Sqrt)
            act.activation(rootn[:, :], rootn[:, :], ACT.Sqrt).then_inc(s_root, 1)
            act.preload_act_table_set("natural_log_exp_and_others")

            def image_exp(turn, n):
                act.wait_ge(s_gd, GATE * turn + 3)
                act.activation(expg[:, 0:n], clamped[:, 0:n], ACT.Exp).then_inc(s_ge, 1)

            def bias_rows(dst, columns):
                for i in range(3):
                    rw = slice(32 * i, 32 * i + 1)
                    act.wait_ge(s_parts, 2 * i + 1)
                    ins = act.activation(dst[rw, :, :], columns(part[i][rw, :]), ACT.Copy)
                ins.then_inc(s_bias, 1)

            act.wait_ge(s_blank, 1)
            bias_rows(bias_o, lambda x: x[:, VD:BR].rearrange("p (t n) -> p t n", t=2))
            image_exp(0, P)
            bias_rows(bias_vd, lambda x: x[:, None, 0:VD].broadcast_to([1, TILES, VD]))

            def step(p, odd, g, ahead, new, cur, old):
                pn, nr, n = at(p, g + 1)
                pc, r, c = at(p, g)
                _, mr, m = at(p, g - 1)

                def copy_turned(c, j):
                    act.wait_ge(s_oTps, TILES * c + j + 1)
                    act.activation(oT[j][:, :], oT_ps, ACT.Copy).then_inc(s_oT, 1)

                def read_o(c, r, j):
                    act.wait_ge(s_ops, TILES * c + j + 1)
                    act.activation(o[r][:, j, :], o_ps, ACT.Copy)
                    act.activation(sq[j][:, :], o_ps, ACT.Square, accum_out=ss[r][:, j:j + 1]).then_inc(s_osq, 1)

                if new:
                    act.wait_ge(s_xTps, n + 1)
                    act.activation(xT[nr][:, :], xT_ps, ACT.Copy).then_inc(s_xT, 1)
                    act.wait_ge(s_qps, n + 1)
                    act.activation(eq[nr][:, :], q_ps, ACT.Exp, bias=col["bq"])
                    act.activation(rq[nr][:, :], q_ps, ACT.Relu, bias=col["bq"]).then_inc(s_qer, 1)
                if old:
                    copy_turned(m, TILES - 1)
                    read_o(m, mr, TILES - 1)
                if new:
                    act.wait_ge(s_kps, n + 1)
                    act.activation(ek[nr][:, :], k_ps, ACT.Exp, bias=col["bk"])
                    act.activation(rk[nr][:, :], k_ps, ACT.Relu, bias=col["bk"]).then_inc(s_ker, 1)
                if cur:
                    copy_turned(c, 0)
                if new:
                    act.wait_ge(s_vps, n + 1)
                    act.activation(ez[nr][:, :, :], v_ps[:, :, D:VD], ACT.Exp, scale=-1.0).then_inc(s_ez, 1)
                if cur:
                    read_o(c, r, 0)
                if new:
                    act.wait_ge(s_lam, 3 * n + 3)
                    act.activation(L[nr][:, :, :], lam[nr][:, :, :], ACT.Ln).then_inc(s_L, 1)
                if gate_here(p, g):
                    image_exp(gate_turn(p, g), P)
                if cur:
                    copy_turned(c, 1)
                if new:
                    act.wait_ge(s_clip, n + 1)
                    act.activation(vp[nr][:, :, :, E], cc[nr][:, :, :], ACT.Exp, scale=-1.0).then_inc(s_dk, 1)
                if cur:
                    read_o(c, r, 1)
                if new:
                    act.wait_ge(s_ktps, n + 1)
                    act.activation(ktok[nr][:, :, :], kt_ps.rearrange("p (t n) -> p t n", t=TILES),
                                   ACT.Copy).then_inc(s_kt, 1)

            over_steps(act, step)

        @block.vector
        def _(dve):
            dve.wait_ge(rows_sem, 32)
            steps = [0]

            def link(ins):
                steps[0] += 1
                ins.then_inc(s_set, 1)
                dve.wait_ge(s_set, steps[0])

            dve.tensor_copy(epsv[:, 0:1], col["eo1"])
            dve.tensor_copy(epsv[:, 1:2], col["eo2"])
            dve.tensor_copy(epsv[:, 2:6], cols[:, COL["ei1a"]:COL["ei1a"] + 4])
            link(dve.tensor_copy(epsv[:, 6:], rows[:, ROW["eo1"][0]:ROW["eo1"][0] + 2 * D]))
            dve.tensor_scalar(roots[:, :], epsv[:, :], 0.0, None, ALU.max)
            dve.tensor_scalar(rootn[:, :], epsv[:, :], -1.0, 0.0, ALU.mult, ALU.max).then_inc(s_root, 1)
            dve.wait_ge(s_root, 2)
            link(dve.tensor_tensor(noise[:, :], roots[:, :], rootn[:, :], ALU.subtract))
            dve.wait_ge(n_sem, 32)
            for layer in range(2):
                eo = noise[:, 6 + D * layer:6 + D * layer + D]
                for kt in range(2):
                    i = 2 * layer + kt
                    dve.scalar_tensor_tensor(nz12[:, i, :], eo, noise[:, 2 + i:3 + i], sw12[:, i, :], ALU.mult, ALU.mult)
                bias_cols = cols[:, COL["b1"] + 3 * layer:COL["b1"] + 3 * layer + 2]
                ins = dve.scalar_tensor_tensor(bias12[:, layer:layer + 1], noise[:, layer:layer + 1], bias_cols[:, 1:2],
                                               bias_cols[:, 0:1], ALU.mult, ALU.add)
            link(ins)
            dve.tensor_tensor(w12[:, :, :], w12[:, :, :], nz12[:, :, :], ALU.add).then_inc(s_noise, 1)
            full = rows[:, 0:BR]
            dve.tensor_copy(part[0][:, :], full).then_inc(s_parts, 1)
            dve.wait_ge(s_parts, 1)
            dve.tensor_tensor(rest[0][:, :], full, part[0][:, :], ALU.subtract).then_inc(s_parts, 1)
            dve.wait_ge(s_parts, 2)
            dve.tensor_copy(part[1][:, :], rest[0][:, :]).then_inc(s_parts, 1)
            dve.wait_ge(s_parts, 3)
            dve.tensor_tensor(rest[1][:, :], rest[0][:, :], part[1][:, :], ALU.subtract).then_inc(s_parts, 1)
            dve.wait_ge(s_parts, 4)
            dve.tensor_copy(part[2][:, :], rest[1][:, :]).then_inc(s_parts, 1)

            def image_reads(turn, n):
                dve.wait_ge(s_gps, turn + 1)
                dve.tensor_scalar(gate[:, 0:n], gate_ps[:, 0:n], bias12[:, 0:1], None, ALU.add).then_inc(s_gd, 1)
                dve.tensor_scalar(inner[:, 0:n], inner_ps[:, 0:n], bias12[:, 1:2], None, ALU.add).then_inc(s_gd, 1)
                dve.wait_ge(s_gd, GATE * turn + 1)
                dve.tensor_scalar(clamped[:, 0:n], gate[:, 0:n], 20.0, None, ALU.min).then_inc(s_gd, 1)

            def image_ratio(turn, n):
                a = GATE * turn
                dve.wait_ge(s_ge, turn + 1)
                dve.scalar_tensor_tensor(num[:, 0:n], expg[:, 0:n], 2.0, expg[:, 0:n], ALU.add, ALU.mult).then_inc(s_gd, 1)
                dve.wait_ge(s_gd, a + 4)
                dve.tensor_scalar(below[:, 0:n], num[:, 0:n], 2.0, None, ALU.add).then_inc(s_gd, 1)
                dve.wait_ge(s_gd, a + 5)
                dve.reciprocal(inv[:, 0:n], below[:, 0:n]).then_inc(s_gd, 1)

            def image_u(turn, n):
                a = GATE * turn
                dve.tensor_tensor(gated[:, 0:n], gate[:, 0:n], inner[:, 0:n], ALU.mult).then_inc(s_gd, 1)
                dve.wait_ge(s_gd, a + 6)
                dve.tensor_tensor(ratio[:, 0:n], num[:, 0:n], inv[:, 0:n], ALU.mult).then_inc(s_gd, 1)
                dve.wait_ge(s_gd, a + 8)
                dve.tensor_tensor(u[:, 0:n], gated[:, 0:n], ratio[:, 0:n], ALU.mult).then_inc(s_gd, 1)

            image_reads(0, P)
            image_ratio(0, P)
            image_u(0, P)
            dve.wait_ge(cst_in_sem, 16)
            dve.wait_ge(s_hps, 1)
            dve.tensor_tensor(h[0][:, 0, :], himg_ps[:, 0:P], cst_of["pos"], ALU.add).then_inc(s_himg, 1)

            def step(p, odd, g, ahead, new, cur, old):
                pn, nr, n = at(p, g + 1)
                pc, r, c = at(p, g)
                _, mr, m = at(p, g - 1)

                def mask(c, r, j):
                    t = TILES * r + j
                    dve.wait_ge(s_sc, TILES * c + j + 1)
                    dve.tensor_tensor(A[j][:, :, :], bankS[t % 2][:, :].rearrange("p (h l) -> p h l", h=H),
                                      cst_of["mask"][:, None, :].broadcast_to([P, H, C]), ALU.mult).then_inc(s_A, 1)

                def norm(c, r, j):
                    T = TILES * c + j
                    nd = nd_ps.rearrange("p (h e) -> p h e", h=H)
                    dve.wait_ge(s_nd, T + 1)
                    dve.scalar_tensor_tensor(den[j][:, :], vp[r][:, j, :, E], DEN_EPS, nd[:, :, E], ALU.mult,
                                             ALU.add).then_inc(s_on, 1)
                    dve.wait_ge(s_on, 3 * T + 1)
                    dve.reciprocal(rden[j][:, :], den[j][:, :]).then_inc(s_on, 1)
                    dve.wait_ge(s_on, 3 * T + 2)
                    dve.tensor_tensor(on[j][:, :].rearrange("p (h e) -> p h e", h=H), nd[:, :, 0:E],
                                      rden[j][:, :, None].broadcast_to([P, H, E]), ALU.mult).then_inc(s_on, 1)

                def copy_state(c, r, j):
                    dve.wait_ge(s_st, TILES * c + j + 1)
                    own = cst_of["blocks"].rearrange("p (b n) -> p b n", b=2)
                    dve.tensor_tensor(S[(j + 1) % TILES][:, :, :].rearrange("p t (b n) -> p t b n", b=2),
                                      state[:, :, None, 0:SB].broadcast_to([P, 2, 2, SB]),
                                      own[:, None, :, :].broadcast_to([P, 2, 2, SB]), ALU.mult).then_inc(s_S, 1)

                def statistics(stat, mv, ve, s, n, src, eps):
                    for j in range(TILES):
                        ins = dve.bn_stats(stat[:, j, :], src[:, j, :])
                    ins.then_inc(s, 1)
                    wait_apart(dve, (s, 3 * n + 1))
                    for j in range(TILES):
                        ins = dve.bn_aggr(mv[:, j, :], stat[:, j, :])
                    ins.then_inc(s, 1)
                    dve.wait_ge(s, 3 * n + 2)
                    dve.tensor_scalar(ve[:, 0, :], mv[:, :, 1], eps, None, ALU.add)
                    dve.tensor_scalar(ve[:, 1, :], mv[:, :, 0], -1.0, None, ALU.mult).then_inc(s, 1)

                if cur:
                    mask(c, r, 1)
                    copy_state(c, r, 0)
                if new:
                    dve.wait_ge(s_qer, n + 1)
                    dve.scalar_tensor_tensor(q[nr][:, :], eq[nr][:, :], 1.0, rq[nr][:, :], ALU.min,
                                             ALU.add).then_inc(s_q, 1)
                if cur:
                    norm(c, r, 0)
                    mask(c, r, 2)
                    copy_state(c, r, 1)
                if ahead:
                    pa, ar, a = at(p, g + 2)
                    ah = h_slot(odd, g + 2)
                    dve.wait_ge(s_hload[ah], 16 * (pa - odd_at(odd, g + 2)) + 32)
                    if ar == 0:
                        dve.wait_ge(s_himg, pa + 1)
                    statistics(stat[ar], mv[ar], ve[ar], s_stat, a, h[ah], LN_EPS)
                if new:
                    dve.wait_ge(s_ker, n + 1)
                    dve.scalar_tensor_tensor(k[nr][:, :], ek[nr][:, :], 1.0, rk[nr][:, :], ALU.min,
                                             ALU.add).then_inc(s_k, 1)
                if old:
                    dve.wait_ge(s_osq, TILES * (m + 1))
                    dve.tensor_scalar(ms[mr][:, :], ss[mr][:, :], 1.0 / D, RMS_EPS, ALU.mult, ALU.add).then_inc(s_ms, 1)
                if new:
                    dve.wait_ge(s_ez, n + 1)
                    dve.tensor_scalar(eu[nr][:, :, :], ez[nr][:, :, :], 1.0, None, ALU.add).then_inc(s_lam, 1)
                    dve.wait_ge(s_lam, 3 * n + 1)
                    dve.reciprocal(er[nr][:, :, :], eu[nr][:, :, :]).then_inc(s_lam, 1)
                    dve.wait_ge(s_lam, 3 * n + 2)
                    dve.tensor_scalar(lam[nr][:, :, :], er[nr][:, :, :], 0.1, 0.9, ALU.mult, ALU.add).then_inc(s_lam, 1)
                if cur:
                    norm(c, r, 1)
                    copy_state(c, r, 2)
                if new:
                    dve.wait_ge(s_L, n + 1)
                    if nr == 0:
                        dve.memset(before[nr][:, 0, :], 0.0).then_inc(s_before, 1)
                    else:
                        dve.tensor_tensor(before[nr][:, 0, :], before[nr - 1][:, TILES - 1, :], L[nr - 1][:, TILES - 1, :],
                                          ALU.add).then_inc(s_before, 1)
                    for j in range(1, TILES):
                        dve.wait_ge(s_before, 3 * n + j)
                        dve.tensor_tensor(before[nr][:, j, :], before[nr][:, j - 1, :], L[nr][:, j - 1, :],
                                          ALU.add).then_inc(s_before, 1)
                if old:
                    dve.wait_ge(s_rr, m + 1)
                    for j in range(TILES):
                        ins = dve.scalar_tensor_tensor(tt[mr][:, j, :], o[mr][:, j, :], rr[mr][:, j:j + 1],
                                                       row_of["ns"], ALU.mult, ALU.mult)
                    ins.then_inc(s_t, 1)
                if gate_here(p, g):
                    image_reads(gate_turn(p, g), P)
                if cur:
                    if g == 0 and h_here(p):
                        wait(dve, s_h2, at(p, GROUPS - H_RING)[2] + 1)
                        dve.wait_ge(s_hps, p + 2)
                        dve.tensor_tensor(h[h_slot(odd, GROUPS)][:, 0, :], himg_ps[:, 0:P], cst_of["pos"],
                                          ALU.add).then_inc(s_himg, 1)
                    norm(c, r, 2)
                if new:
                    dve.wait_ge(s_cum, n + 1)
                    dve.tensor_scalar(cc[nr][:, :, :], cum_ps.rearrange("p (t h) -> p t h", t=TILES), -50.0, 50.0,
                                      ALU.max, ALU.min).then_inc(s_clip, 1)
                    dve.wait_ge(s_dk, n + 1)
                    dve.tensor_tensor(vp[nr][:, :, :, 0:E], v_ps[:, :, 0:D].rearrange("p t (h e) -> p t h e", h=H),
                                      vp[nr][:, :, :, E:W1E].broadcast_to([P, TILES, H, E]), ALU.mult).then_inc(s_vp, 1)
                if gate_here(p, g):
                    image_ratio(gate_turn(p, g), P)
                if new:
                    mask(n, nr, 0)
                if old:
                    dve.wait_ge(s_h2, m + 1)
                    statistics(stat2[mr], mv2[mr], ve2[mr], s_st2, m, h2[mr], LN_EPS)
                if gate_here(p, g):
                    image_u(gate_turn(p, g), P)

            over_steps(dve, step)

        @block.gpsimd
        def _(pool):
            pool.memset(ones_b[:, :], 1.0)
            pool.memset(bias_vd[:, :, :], 0.0)
            pool.memset(bias_o[:, :, :], 0.0).then_inc(s_blank, 1)
            for r in range(GROUPS):
                ins = pool.memset(qbd[r][:, :, :], 0.0)
            ins.then_inc(s_zero, 1)
            pool.memset(minus_half[:, :], -0.5).then_inc(s_zero, 1)
            pool.wait_ge(s_zero, 2)

            def step(p, odd, g, ahead, new, cur, old):
                pa, ar, a = at(p, g + 2)
                ah = h_slot(odd, g + 2)
                pm, mr, m = at(p, g - 1)
                mh = h_slot(odd, g - 1)
                if ahead:
                    pool.wait_ge(s_stat, 3 * a + 3)
                    pool.tensor_tensor(rn[ar][:, 0, :], ve[ar][:, 0, :], minus_half[:, :], ALU.pow).then_inc(s_ln, 1)
                    pool.wait_ge(s_ln, 3 * a + 1)
                    pool.tensor_tensor(rn[ar][:, 1, :], ve[ar][:, 1, :], rn[ar][:, 0, :], ALU.mult).then_inc(s_ln, 1)
                    wait_apart(pool, (s_ln, 3 * a + 2))
                    for j in range(TILES):
                        ins = pool.tensor_scalar(xn[ar][:, j, :], h[ah][:, j, :], rn[ar][:, 0, j:j + 1],
                                                 rn[ar][:, 1, j:j + 1], ALU.mult, ALU.add)
                    ins.then_inc(s_ln, 1)
                if old:
                    pool.wait_ge(s_ms, m + 1)
                    pool.tensor_tensor(rr[mr][:, :], ms[mr][:, :], minus_half[:, :], ALU.pow).then_inc(s_rr, 1)
                    pool.wait_ge(s_t, m + 1)
                    pool.tensor_tensor(h2[mr][:, :, :], h[mh][:, :, :], tt[mr][:, :, :], ALU.add).then_inc(s_h2, 1)
                if old:
                    pool.wait_ge(s_st2, 3 * m + 3)
                    pool.tensor_tensor(rn2[mr][:, 0, :], ve2[mr][:, 0, :], minus_half[:, :], ALU.pow).then_inc(s_rn2, 1)
                    pool.wait_ge(s_rn2, 3 * m + 1)
                    pool.tensor_tensor(rn2[mr][:, 1, :], ve2[mr][:, 1, :], rn2[mr][:, 0, :], ALU.mult).then_inc(s_rn2, 1)
                    pool.tensor_scalar(sc2[mr][:, :], rn2[mr][:, 0, :], 1.0, None, ALU.add).then_inc(s_rn2, 1)
                if old:
                    wait_apart(pool, (s_rn2, 3 * m + 3), (s_out[mr], 32 * pm))
                    for j in range(TILES):
                        ins = pool.tensor_scalar(y[mr][:, j, :], h2[mr][:, j, :], sc2[mr][:, j:j + 1],
                                                 rn2[mr][:, 1, j:j + 1], ALU.mult, ALU.add)
                    ins.then_inc(s_y, 1)

            over_steps(pool, step)
    return nc


def _constants():
    s = np.arange(P)
    same = (s[:, None] // C) == (s[None, :] // C)
    U = (same & (s[:, None] <= s[None, :])).astype(np.float32)
    ones = same.astype(np.float32)
    ident = np.eye(P, dtype=np.float32)
    mask = ((s[:, None] % C) <= np.arange(C)[None, :]).astype(np.float32)
    blocks = ((s[:, None] // E) == (np.arange(SV)[None, :] // W1E)).astype(np.float32)
    div = np.exp(np.arange(0, D, 2, dtype=np.float32) * np.float32(-np.log(10000.0) / D)).astype(np.float32)
    ang = np.arange(C, dtype=np.float32)[:, None] * div
    pos = np.stack([np.sin(ang), np.cos(ang)], axis=-1).reshape(C, D).astype(np.float32)
    return np.concatenate([U, ones, ident, mask, blocks, np.concatenate([pos, pos])], axis=1)


def kernel(**inputs):
    import concourse.bacc as _bacc
    from concourse.bass_utils import run_bass_kernel_spmd as _run

    a = {n: np.asarray(v) for n, v in inputs.items()}
    w = lambda n: a["L0_" + n]
    x = a["x"].reshape(BATCHES, 8, 16, 8, 16).transpose(2, 4, 0, 1, 3).reshape(2, P, BATCHES * C).transpose(1, 0, 2)
    qkv = w("attn_qkv_w")
    wts = np.concatenate([qkv[0:D].T, qkv[D:2 * D].T, qkv[2 * D:3 * D].T, w("attn_decay_w").T, w("attn_out_w").T,
                          w("tok_W3_w").T], axis=1)
    by_pixel = lambda m: m.T.reshape(2, P, D).transpose(1, 0, 2)
    noisy_w = np.concatenate([by_pixel(w("tok_W1_w")), by_pixel(w("tok_W2_w"))], axis=1)
    noisy_sw = np.concatenate([by_pixel(w("tok_W1_sw")), by_pixel(w("tok_W2_sw"))], axis=1)
    qkv_b = w("attn_qkv_b")
    cols = np.stack([qkv_b[0:D], qkv_b[D:2 * D], w("tok_W1_b"), w("tok_W1_sb"), w("tok_eps_out1"), w("tok_W2_b"),
                     w("tok_W2_sb"), w("tok_eps_out2"), w("tok_eps_in1")[0:P], w("tok_eps_in1")[P:],
                     w("tok_eps_in2")[0:P], w("tok_eps_in2")[P:]], axis=1)
    rows = np.concatenate([qkv_b[2 * D:3 * D], w("attn_decay_b"), w("attn_out_b"), w("tok_W3_b"),
                           w("attn_norm_scale"), w("tok_eps_out1"), w("tok_eps_out2")])[None, :]
    arrays = {"txt": a["txt"], "patches": x, "constants": _constants(), "weights": wts, "noisy_w": noisy_w,
              "noisy_sw": noisy_sw, "columns": cols, "rows": rows}
    nc = _bacc.Bacc("TRN2", target_bir_lowering=False, num_devices=1)
    args = []
    for name in arrays:
        arrays[name] = np.ascontiguousarray(arrays[name])
        args.append(nc.dram_tensor(f"in_{name}", arrays[name].shape, mybir.dt.from_np(arrays[name].dtype),
                                   kind="ExternalInput").ap())
    args.append(nc.dram_tensor("result", (BATCHES, C + TEXT, D), F32, kind="ExternalOutput").ap())
    build(nc, *args)
    r = _run(nc, [{f"in_{n}": v for n, v in arrays.items()}], core_ids=[0])
    return r.results[0]["result"]
```
